# Optimizing a Trainium2 kernel written in Bass

```python
import numpy as np
import jax
import jax.numpy as jnp

def _softmax(x, axis=-1):
    return jax.nn.softmax(x, axis=axis)

def _gelu(x):
    return jax.nn.gelu(x, approximate=True)

def _silu(x):
    return jax.nn.silu(x)

def _sigmoid(x):
    return jax.nn.sigmoid(x)

def _layernorm(x, axis=-1, eps=1e-05):
    m = jnp.mean(x, axis=axis, keepdims=True)
    v = jnp.var(x, axis=axis, keepdims=True)
    return (x - m) / jnp.sqrt(v + eps)

def _scatter_add(tgt, idx, src, axis=0):
    return tgt.at[idx].add(src)

def _segment_sum(src, seg, n):
    return jax.ops.segment_sum(src, seg, n)
kernel_name = 'mk_sandwich_d1_jaxref_r8_2fe901'

def setup_inputs(seed: int=0):
    np.random.seed(seed)
    _w = jnp.asarray

    def _L0_attn_setup():
        import jax, jax.numpy as jnp
        import numpy as np
        DIM = 128
        HEADS = 16
        HEAD_DIM = DIM // HEADS
        THRESH = 0.29514
        SHARP = 15.0
        LN_EPS = 1e-05
        NORM_EPS = 1e-12

        def _l2norm(t):
            n = jnp.sqrt(jnp.sum(t * t, axis=-1, keepdims=True))
            return t / jnp.maximum(n, NORM_EPS)
        key = jax.random.key(seed)
        ks = jax.random.split(key, 8)
        s = 1.0 / np.sqrt(DIM)
        sg = 1.0 / np.sqrt(HEAD_DIM)
        return {'x': jax.random.normal(ks[0], (2, 256, DIM), dtype=jnp.float32), 'Wq': jax.random.uniform(ks[1], (DIM, DIM), jnp.float32, -s, s), 'Wk': jax.random.uniform(ks[2], (DIM, DIM), jnp.float32, -s, s), 'Wv': jax.random.uniform(ks[3], (DIM, DIM), jnp.float32, -s, s), 'gq': jax.random.uniform(ks[4], (HEAD_DIM,), jnp.float32, -sg, sg), 'gk': jax.random.uniform(ks[5], (HEAD_DIM,), jnp.float32, -sg, sg), 'Wo': jax.random.uniform(ks[6], (DIM, DIM), jnp.float32, -s, s), 'bo': jax.random.uniform(ks[7], (DIM,), jnp.float32, -s, s), 'ln_w': jnp.ones((DIM,), jnp.float32), 'ln_b': jnp.zeros((DIM,), jnp.float32)}
    _L0_attn_in = _L0_attn_setup()

    def _L0_ffn_setup():
        import jax, jax.numpy as jnp
        import numpy as np
        B, S, D, F, E, K = (4, 256, 128, 512, 8, 2)
        FS = 128
        LN_EPS = 1e-05

        def _swiglu(x, gu_w, dn_w):
            gate, up = jnp.split(x @ gu_w, 2, axis=-1)
            gate = jnp.clip(gate, -10.0, 10.0)
            return jax.nn.silu(gate) * up @ dn_w
        key = jax.random.key(seed)
        ks = jax.random.split(key, 6)
        s = 0.02
        return {'x': jax.random.normal(ks[0], (B, S, D), jnp.float32), 'ln_gamma': jnp.ones((D,), jnp.float32), 'ln_beta': jnp.zeros((D,), jnp.float32), 'router_w': jax.random.normal(ks[1], (D, E), jnp.float32) * s, 'gate_up_w': jax.random.normal(ks[2], (E, D, 2 * F), jnp.float32) * s, 'down_w': jax.random.normal(ks[3], (E, F, D), jnp.float32) * s, 'shared_gate_up_w': jax.random.normal(ks[4], (D, 2 * FS), jnp.float32) * s, 'shared_down_w': jax.random.normal(ks[5], (FS, D), jnp.float32) * s}
    _L0_ffn_in = _L0_ffn_setup()
    _d = {'L0_attn_x': _L0_attn_in['x'], 'L0_attn_Wq': _L0_attn_in['Wq'], 'L0_attn_Wk': _L0_attn_in['Wk'], 'L0_attn_Wv': _L0_attn_in['Wv'], 'L0_attn_gq': _L0_attn_in['gq'], 'L0_attn_gk': _L0_attn_in['gk'], 'L0_attn_Wo': _L0_attn_in['Wo'], 'L0_attn_bo': _L0_attn_in['bo'], 'L0_attn_ln_w': _L0_attn_in['ln_w'], 'L0_attn_ln_b': _L0_attn_in['ln_b'], 'L0_ffn_ln_gamma': _L0_ffn_in['ln_gamma'], 'L0_ffn_ln_beta': _L0_ffn_in['ln_beta'], 'L0_ffn_router_w': _L0_ffn_in['router_w'], 'L0_ffn_gate_up_w': _L0_ffn_in['gate_up_w'], 'L0_ffn_down_w': _L0_ffn_in['down_w'], 'L0_ffn_shared_gate_up_w': _L0_ffn_in['shared_gate_up_w'], 'L0_ffn_shared_down_w': _L0_ffn_in['shared_down_w']}
    _x0 = _d['L0_attn_x']
    _d['L0_attn_x'] = jax.random.normal(jax.random.fold_in(jax.random.key(seed), 1), (1, 2048, 128), dtype=_x0.dtype)
    del _x0
    return _d

def reference(L0_attn_x, L0_attn_Wq, L0_attn_Wk, L0_attn_Wv, L0_attn_gq, L0_attn_gk, L0_attn_Wo, L0_attn_bo, L0_attn_ln_w, L0_attn_ln_b, L0_ffn_ln_gamma, L0_ffn_ln_beta, L0_ffn_router_w, L0_ffn_gate_up_w, L0_ffn_down_w, L0_ffn_shared_gate_up_w, L0_ffn_shared_down_w):

    def _L0_attn_ref(x, Wq, Wk, Wv, gq, gk, Wo, bo, ln_w, ln_b):
        import jax, jax.numpy as jnp
        import numpy as np
        DIM = 128
        HEADS = 16
        HEAD_DIM = DIM // HEADS
        THRESH = 0.29514
        SHARP = 15.0
        LN_EPS = 1e-05
        NORM_EPS = 1e-12

        def _l2norm(t):
            n = jnp.sqrt(jnp.sum(t * t, axis=-1, keepdims=True))
            return t / jnp.maximum(n, NORM_EPS)
        B, T, D = x.shape
        mu = jnp.mean(x, axis=-1, keepdims=True)
        var = jnp.mean((x - mu) ** 2, axis=-1, keepdims=True)
        x_norm = (x - mu) / jnp.sqrt(var + LN_EPS) * ln_w + ln_b

        def split_heads(t):
            return t.reshape(B, T, HEADS, HEAD_DIM).transpose(0, 2, 1, 3)
        q = _l2norm(split_heads(x_norm @ Wq))
        k = _l2norm(split_heads(x_norm @ Wk))
        v = split_heads(x @ Wv)
        align = jnp.einsum('bhtd,bhsd->bhts', q, k)
        resonance = jax.nn.sigmoid((align - THRESH) * SHARP)
        gate_q = jnp.einsum('bhtd,d->bht', q, gq)
        gate_k = jnp.einsum('bhsd,d->bhs', k, gk)
        modulation = resonance * gate_q[..., :, None] * gate_k[..., None, :]
        collapse = jnp.einsum('bhts,bhsd->bhtd', modulation, v)
        collapse = collapse.transpose(0, 2, 1, 3).reshape(B, T, D)
        return collapse @ Wo + bo

    def _L0_ffn_ref(x, ln_gamma, ln_beta, router_w, gate_up_w, down_w, shared_gate_up_w, shared_down_w):
        import jax, jax.numpy as jnp
        import numpy as np
        B, S, D, F, E, K = (4, 256, 128, 512, 8, 2)
        FS = 128
        LN_EPS = 1e-05

        def _swiglu(x, gu_w, dn_w):
            gate, up = jnp.split(x @ gu_w, 2, axis=-1)
            gate = jnp.clip(gate, -10.0, 10.0)
            return jax.nn.silu(gate) * up @ dn_w
        b, s, d = x.shape
        xf = x.reshape(-1, d)
        mu = jnp.mean(xf, axis=-1, keepdims=True)
        var = jnp.var(xf, axis=-1, keepdims=True)
        xn = (xf - mu) * jax.lax.rsqrt(var + LN_EPS) * ln_gamma + ln_beta
        logits = xn @ router_w
        probs = jax.nn.softmax(logits, axis=-1)
        topv, topi = jax.lax.top_k(probs, K)
        topv = topv / jnp.sum(topv, axis=-1, keepdims=True)
        comb = jnp.sum(jax.nn.one_hot(topi, E, dtype=xn.dtype) * topv[..., None], axis=1)
        out = jnp.zeros_like(xf)
        for e in range(E):
            out = out + comb[:, e:e + 1] * _swiglu(xn, gate_up_w[e], down_w[e])
        out = out + _swiglu(xn, shared_gate_up_w, shared_down_w)
        return out.reshape(b, s, d)
    x = L0_attn_x
    x = x + _layernorm(_L0_attn_ref(_layernorm(x, axis=-1), L0_attn_Wq, L0_attn_Wk, L0_attn_Wv, L0_attn_gq, L0_attn_gk, L0_attn_Wo, L0_attn_bo, L0_attn_ln_w, L0_attn_ln_b), axis=-1)
    x = x + _layernorm(_L0_ffn_ref(_layernorm(x, axis=-1), L0_ffn_ln_gamma, L0_ffn_ln_beta, L0_ffn_router_w, L0_ffn_gate_up_w, L0_ffn_down_w, L0_ffn_shared_gate_up_w, L0_ffn_shared_down_w), axis=-1)
    return x

_drawn_inputs = setup_inputs


def setup_inputs(seed=0):
    import zlib

    import numpy as np

    out = dict(_drawn_inputs(seed))
    spreads = {'L0_attn_ln_w': (1.0, 0.2),
     'L0_attn_ln_b': (0.0, 0.1),
     'L0_ffn_ln_gamma': (1.0, 0.2),
     'L0_ffn_ln_beta': (0.0, 0.1)}
    factors = {}
    for name, (base, spread) in spreads.items():
        noise = np.random.default_rng([zlib.crc32(name.encode()), seed]).standard_normal(out[name].shape)
        drawn = base * np.exp(spread * noise) if base else spread * noise
        out[name] = jnp.asarray(drawn.astype(out[name].dtype))
    for name, factor in factors.items():
        out[name] = (out[name] * factor).astype(out[name].dtype)
    return out
```

```python
from contextlib import ExitStack

import concourse.bass as bass
from concourse import mybir

P = 128
T = 2048
D = 128
H = 16
HD = D // H
SLOTS = 4
G = 4
NG = H // G
TB = 512
SUB = TB // P
NB = T // TB
ST = T // P
E = 8
F = 512
FC = F // P
NCH = E * FC + 1
GU = E * 2 * F + 2 * P
ROUNDS = NG * ST
SPL = 1024
NSPL = -(-GU // SPL)

THRESH, SHARP, EPS, NORM_EPS = 0.29514, 15.0, 1e-5, 1e-12
QK_SCALE = 64.0
RSQRT_MAGIC = 1597463007.0

F32 = mybir.dt.float32
F32R = mybir.dt.float32r
F16 = mybir.dt.float16
BF16 = mybir.dt.bfloat16
I32 = mybir.dt.int32
U32 = mybir.dt.uint32
ALU = mybir.AluOpType
ACT = mybir.ActivationFunctionType
AX_X = mybir.AxisListType.X

C_ID, C_MA, C_MB, C_IO = 0, P, 2 * P, 3 * P
V_LNW, V_LNB, V_GAM, V_BET, V_GQ, V_GK, V_BO = 0, 1, 2, 3, 4, 5, 5 + HD
NCONST, NVEC = 3 * P + E, 5 + HD + D

PRO_STEPS = 53
BLK_STEPS = 105


COMB_CHUNK = 1


def chunk_round(c):
    return 7 + int(c * 1.6)


COMB_ROUND = chunk_round(COMB_CHUNK)


def build(nc, x, wqkv, vecs, consts, ident16, wo, router, gu, down, out):
    ctx = ExitStack()
    with ctx:
        def sb(name, shape, dt=F32):
            return ctx.enter_context(nc.sbuf_tensor(name, shape, dt))

        def sem(name):
            return ctx.enter_context(nc.semaphore(name))

        x_sb = sb("x_sb", [P, ST, D])
        const_sb = sb("const_sb", [P, NCONST])
        vec_sb = sb("vec_sb", [P, NVEC])
        id16 = sb("id16", [P, P], F16)
        w_qkv = sb("w_qkv", [P, 3 * D])
        wo_sb = sb("wo_sb", [P, NG, D])
        rw_sb = sb("rw_sb", [P, E])
        lnb_all = sb("lnb_all", [P, P])
        b_qk = sb("b_qk", [P, 2 * D])
        gu_hi = sb("gu_hi", [P, GU], F32R)
        gu_lo = sb("gu_lo", [P, GU], F32R)
        down_sb = sb("down_sb", [P, NCH, D])
        vg = sb("vg", [P, ST, H, HD])
        kT = sb("kT", [P, NG, T], F16)
        qT = sb("qT", [P, NG, TB], F16)
        q_pad = sb("q_pad", [P, NG, G, TB], F16)
        res = sb("res", [P, 2, G, TB])
        coll = sb("coll", [P, NG, TB])
        gate_q = sb("gate_q", [P, TB])
        gq_parts = sb("gq_parts", [P, 8])
        gq16 = sb("gq16", [P, 3], BF16)
        gm_a = sb("gm_a", [P, P], BF16)
        gm_b = sb("gm_b", [P, P], BF16)
        gm_t = sb("gm_t", [P, P])
        sig_bias = sb("sig_bias", [P, 1])
        tok = sb("tok", [P, SUB, D])
        xn_hi = sb("xn_hi", [P, TB], F32R)
        xn_lo = sb("xn_lo", [P, TB], F32R)
        comb_all = sb("comb_all", [P, 2, TB])
        bst = sb("bst", [P, SUB, 6])
        mv = sb("mv", [P, SUB, 2])
        small = sb("small", [P, 8, SUB])
        logit = sb("logit", [P, SUB, E])
        top = sb("top", [P, SUB, 8])
        topi = sb("topi", [P, SUB, 8], U32)
        topf = sb("topf", [P, SUB, 2])
        pause = sb("pause", [P, 1])
        tdiff = sb("tdiff", [P, SUB])
        twt = sb("twt", [P, 2, SUB])
        hot = sb("hot", [P, 3, SUB, E])
        work = sb("work", [P, 12 * TB])
        gate_c = [work[:, n * TB:(n + 1) * TB] for n in (0, 1)]
        prod = [work[:, n * TB:(n + 1) * TB] for n in (2, 3)]
        sg = [work[:, n * TB:(n + 1) * TB] for n in (4, 5)]
        hid = [work[:, n * TB:(n + 1) * TB] for n in (6, 7)]
        x1 = work[:, 8 * TB:9 * TB].rearrange("p (s d) -> p s d", s=SUB)
        acc = work[:, 9 * TB:10 * TB]
        tmp = work[:, 10 * TB:11 * TB]
        xnT = work[:, 11 * TB:12 * TB]
        combT = tmp[0:E, :]
        raw_w = [work[:, n * SPL:(n + 1) * SPL] for n in (0, 1)]
        hT = work[:, 0:TB]
        raw = work[:, TB:4 * TB].rearrange("p (s n) -> p s n", s=SUB)
        qk = work[:, 4 * TB:6 * TB].rearrange("p (w n) -> p w n", w=2)
        sq = work[:, 6 * TB:8 * TB].rearrange("p (n d) -> p n d", d=HD)
        split = work[:, 8 * TB:12 * TB].bitcast(F16).rearrange(
            "p (w n s d) -> p w n s d", w=2, s=SLOTS, d=HD)
        ssq = sb("ssq", [P, 2, SUB * H])
        rn = sb("rn", [P, 2 * SUB * H])
        rn_t = sb("rn_t", [P, 2 * SUB * H])
        gk_s = sb("gk_s", [P, SUB * H])

        q_dram = nc.dram_tensor("q_dram", (NB, P, NG, TB), F16).ap()
        comb_dram = nc.dram_tensor("comb_dram", (E, TB), F32).ap()

        S = ctx.enter_context(nc.psum_tensor("S", [P, G, TB], F32))
        AV = ctx.enter_context(nc.psum_tensor("AV", [P, TB], F32))
        GB = ctx.enter_context(nc.psum_tensor("GB", [P, TB], F32))
        UB = ctx.enter_context(nc.psum_tensor("UB", [P, TB], F32))
        OB = ctx.enter_context(nc.psum_tensor("OB", [P, TB], F32))

        ident = const_sb[:, C_ID:C_ID + P]
        iota = const_sb[:, C_IO:C_IO + E]

        def col(n):
            return vec_sb[:, n:n + 1]

        in_x = sem("in_x")
        in_w = sem("in_w")
        in_down = sem("in_down")
        in_raw = [sem("in_raw0"), sem("in_raw1")]
        zeroed = sem("zeroed")
        setup = sem("setup")
        bias_mm = sem("bias_mm")
        pro = sem("pro")
        h_ready = sem("h_ready")
        hT_mm = sem("hT_mm")
        hT_ready = sem("hT_ready")
        qkv_mm = sem("qkv_mm")
        raw_ready = sem("raw_ready")
        qk_ready = sem("qk_ready")
        sq_ready = sem("sq_ready")
        unit_ready = sem("unit_ready")
        hi_ready = sem("hi_ready")
        lo_ready = sem("lo_ready")
        vg_ready = sem("vg_ready")
        qk_tr = sem("qk_tr")
        qk_copied = sem("qk_copied")
        q_saved = sem("q_saved")
        q_staged = [sem(f"q_staged{g}") for g in range(NG)]
        w_hi = sem("w_hi")
        w_lo = sem("w_lo")
        score_mm = sem("score_mm")
        sig_done = sem("sig_done")
        av_mm = sem("av_mm")
        gateb_mm = sem("gateb_mm")
        gateb_copied = sem("gateb_copied")
        coll_ready = sem("coll_ready")
        proj_mm = sem("proj_mm")
        blk = sem("blk")
        n2_ready = sem("n2_ready")
        n2_mm = sem("n2_mm")
        xn_ready = sem("xn_ready")
        router_mm = sem("router_mm")
        diff_ready = sem("diff_ready")
        twt_ready = sem("twt_ready")
        comb_ready = sem("comb_ready")
        combT_mm = sem("combT_mm")
        combT_ready = sem("combT_ready")
        comb_saved = sem("comb_saved")
        comb_in = [sem("comb_in0"), sem("comb_in1")]
        gate_mm = sem("gate_mm")
        up_mm = sem("up_mm")
        gate_clipped = sem("gate_clipped")
        prod_ready = sem("prod_ready")
        sg_ready = sem("sg_ready")
        hid_ready = sem("hid_ready")
        down_mm = sem("down_mm")
        acc_ready = sem("acc_ready")
        fin_mm = sem("fin_mm")
        fin_read = sem("fin_read")
        out_ready = sem("out_ready")
        out_saved = sem("out_saved")

        def rsqrt(link, v, y, t):
            link(nc.vector.tensor_scalar(t.bitcast(I32), v.bitcast(I32), 1, None, ALU.logical_shift_right))
            link(nc.vector.tensor_scalar(y.bitcast(I32), t.bitcast(I32), -1.0, RSQRT_MAGIC, ALU.mult, ALU.add))
            for _ in range(3):
                link(nc.vector.scalar_tensor_tensor(out=t, in0=y, scalar=-0.5, in1=y, op0=ALU.mult, op1=ALU.mult))
                link(nc.vector.tensor_tensor(t, t, v, ALU.mult))
                link(nc.vector.scalar_tensor_tensor(out=y, in0=t, scalar=1.5, in1=y, op0=ALU.add, op1=ALU.mult))

        class Steps:

            def __init__(self, eng, s, base):
                self.eng, self.s, self.base, self.n = eng, s, base, 0

            def count(self, ins):
                self.n += 1
                ins.then_inc(self.s, 1)

            def __call__(self, ins, alone=False):
                self.count(ins)
                self.eng.wait_ge(self.s, self.base + self.n)
                if alone:
                    self.eng.memset(pause[:], 0.0)

        def wait(eng, s, value):
            if not isinstance(value, int) or value > 0:
                eng.wait_ge(s, value)

        block = ctx.enter_context(nc.Block())

        @block.sync
        def _(sp):
            for j in range(NB):
                sp.dma_start(x_sb[:, j * SUB:(j + 1) * SUB, :], x[:, j * SUB:(j + 1) * SUB, :]).then_inc(in_x, 16)
            for dst, src in ((const_sb, consts), (vec_sb, vecs), (id16, ident16), (w_qkv, wqkv),
                             (wo_sb, wo), (rw_sb, router)):
                sp.dma_start(dst[:], src).then_inc(in_w, 16)
            sp.dma_start(down_sb[:], down).then_inc(in_down, 16)
            with sp.Fori(0, NB) as i:
                sp.wait_ge(qk_copied, i * 4 + 2)
                sp.dma_start(q_dram[bass.ds(i, 1)].rearrange("o p g t -> (o p) g t"), qT[:]).then_inc(q_saved, 16)
            sp.wait_ge(q_saved, 16 * NB)
            sp.wait_ge(qk_copied, 4 * NB)
            sp.wait_ge(vg_ready, NB)
            for n in range(NSPL):
                w = min(SPL, GU - n * SPL)
                if n >= 2:
                    sp.wait_ge(w_lo, n - 1)
                sp.dma_start(raw_w[n % 2][:, 0:w], gu[:, n * SPL:n * SPL + w]).then_inc(in_raw[n % 2], 16)

            def experts(i):
                sp.wait_ge(combT_ready, i)
                sp.dma_start(comb_dram, combT).then_inc(comb_saved, 16)
                sp.wait_ge(comb_saved, i * 16)
                for e in range(E):
                    if e >= 2:
                        sp.wait_ge(acc_ready, (i - 1) * (E + 1) + e - 1)
                    sp.dma_start(comb_all[:, e % 2, :], comb_dram[e, :].partition_broadcast(P)).then_inc(comb_in[e % 2], 16)
                sp.wait_ge(out_ready, i)
                sp.dma_start(out[:, bass.ds((i - 1) * SUB, SUB), :], tok[:]).then_inc(out_saved, 16)

            with sp.Fori(1, NB) as i:
                experts(i)
            experts(NB)
            sp.wait_ge(out_saved, 16 * NB)
            for g in range(NG):
                sp.wait_ge(q_staged[g], (NB + 1) * 5 * 16)

        @block.gpsimd
        def _(pool):
            nc.gpsimd.memset(q_pad[:].rearrange("p g j t -> p (g j t)").bitcast(F32), 0.0).then_inc(zeroed, 1)
            for n in range(NSPL):
                a, w = n * SPL, min(SPL, GU - n * SPL)
                pool.wait_ge(in_raw[n % 2], 16 * (n // 2 + 1))
                nc.gpsimd.tensor_scalar(gu_hi[:, a:a + w], raw_w[n % 2][:, 0:w], 1.0, 0.0, ALU.mult, ALU.add).then_inc(w_hi, 1)
                pool.wait_ge(w_hi, n + 1)
                nc.gpsimd.tensor_tensor(gu_lo[:, a:a + w], raw_w[n % 2][:, 0:w], gu_hi[:, a:a + w].bitcast(F32),
                                        ALU.subtract).then_inc(w_lo, 1)

            def experts(i):
                for c in range(NCH):
                    n = (i - 1) * NCH + c
                    pool.wait_ge(prod_ready, n + 1)
                    pool.wait_ge(sg_ready, n + 1)
                    wait(pool, down_mm, n - 1 if c >= 2 or not isinstance(i, int) or i > 1 else 0) if c >= 2 else (
                        pool.wait_ge(down_mm, (i - 1) * NCH))
                    nc.gpsimd.tensor_tensor(hid[c % 2], prod[c % 2], sg[c % 2], ALU.mult).then_inc(hid_ready, 1)

            with pool.Fori(1, NB) as i:
                experts(i)
            experts(NB)

        @block.scalar
        def _(act):
            with act.Fori(0, NB) as i:
                act.wait_ge(hT_mm, i + 1)
                nc.scalar.activation(hT, UB[:], ACT.Copy).then_inc(hT_ready, 1)
                for j in range(SUB):
                    act.wait_ge(qkv_mm, i * SUB + j + 1)
                    nc.scalar.activation(raw[:, j, :], (GB, OB)[j % 2][:, 0:3 * D], ACT.Copy).then_inc(raw_ready, 1)
                act.wait_ge(qk_ready, i * SUB + SUB)
                nc.scalar.activation(sq, qk.rearrange("p w n -> p (w n)").rearrange("p (n d) -> p n d", d=HD),
                                     ACT.Square).then_inc(sq_ready, 1)
                act.wait_ge(unit_ready, i + 1)
                for w, slots in ((0, slice(0, 3, 2)), (1, slice(0, 2))):
                    for part in (0, 1):
                        s = slots.start + part * (slots.step or 1)
                        nc.scalar.activation(split[:, w, :, s, :], qk[:, w, :].rearrange("p (n d) -> p n d", d=HD),
                                             ACT.Copy).then_inc(hi_ready, 1)
                for b in range(4):
                    dst = qT[:] if b < 2 else kT[:, :, bass.ds(i * TB, TB)]
                    g = 2 * (b % 2)
                    if b == 0:
                        act.wait_ge(q_saved, i * 16)
                    act.wait_ge(qk_tr, i * 4 + b + 1)
                    nc.scalar.activation(dst[:, g:g + 2, :], (UB, OB)[b % 2][:].bitcast(F16).rearrange("p (g t) -> p g t", g=2),
                                         ACT.Copy).then_inc(qk_copied, 1)
            act.wait_ge(q_saved, 16 * NB)
            act.wait_ge(zeroed, 1)

            def stage(b, g):
                src = q_dram[bass.ds(b, 1)].rearrange("o p g t -> (o p) g t") if not isinstance(b, int) else q_dram[b]
                for j in range(G):
                    r = slice(32 * j, 32 * j + 32)
                    act.dma_start(q_pad[r, g, j, :], src[r, g, :]).then_inc(q_staged[g], 16)
                act.dma_start(qT[:, g, :], src[:, g, :]).then_inc(q_staged[g], 16)

            for g in range(NG):
                stage(0, g)

            def silu(i, c):
                n = (i - 1) * NCH + c
                act.wait_ge(gate_clipped, n + 1)
                if c >= 2:
                    act.wait_ge(hid_ready, n - 1)
                nc.scalar.activation(sg[c % 2], gate_c[c % 2], ACT.Sigmoid).then_inc(sg_ready, 1)

            def top_weights(i):
                act.wait_ge(diff_ready, i)
                nc.scalar.activation(twt[:, 0, :], tdiff[:], ACT.Sigmoid, scale=-1.0).then_inc(twt_ready, 1)
                nc.scalar.activation(twt[:, 1, :], tdiff[:], ACT.Sigmoid).then_inc(twt_ready, 1)

            def rounds(i, experts):
                for k in range(ROUNDS):
                    for half in (0, 1):
                        act.wait_ge(score_mm, i * 2 * ROUNDS + 2 * k + half + 1)
                        if half == 0:
                            wait(act, av_mm, i * ROUNDS + k - 1)
                        nc.scalar.activation(
                            res[:, k % 2, 2 * half:2 * half + 2, :].rearrange("p h t -> p (h t)"),
                            S[:, 2 * half:2 * half + 2, :].rearrange("p h t -> p (h t)"), ACT.Sigmoid,
                            bias=sig_bias[:, 0:1], scale=SHARP / (QK_SCALE * QK_SCALE)).then_inc(sig_done, 1)
                    g, s = k // ST, k % ST
                    if s == 10:
                        act.wait_ge(gateb_mm, i * NG + g + 1)
                        wait(act, coll_ready, i * NG + g)
                        nc.scalar.activation(gate_q[:], GB[:], ACT.Copy, scale=1.0 / QK_SCALE).then_inc(gateb_copied, 1)
                    if s == 1 and g > 0:
                        act.wait_ge(score_mm, i * 2 * ROUNDS + 2 * g * ST)
                        act.wait_ge(gateb_mm, i * NG + g)
                        stage((i + 1) % NB, g - 1)
                    if experts:
                        if k == 7:
                            top_weights(i)
                        for c in range(NCH):
                            if chunk_round(c) == k:
                                silu(i, c)
                act.wait_ge(gateb_mm, i * NG + NG)
                stage((i + 1) % NB, NG - 1)

            act.wait_ge(setup, 1)
            rounds(0, False)
            with act.Fori(1, NB) as i:
                rounds(i, True)
            top_weights(NB)
            for c in range(NCH):
                silu(NB, c)

        @block.tensor
        def _(pe):
            pe.wait_ge(in_w, 6 * 16)
            pe.wait_ge(setup, 3)
            nc.tensor.matmul(GB[:, 0:2 * D], lnb_all[:], w_qkv[:, 0:2 * D], start=True, stop=True).then_inc(bias_mm, 1)
            pe.wait_ge(setup, 5)
            with pe.Fori(0, NB) as i:
                pe.wait_ge(h_ready, i * SUB + SUB)
                pe.wait_ge(qk_copied, i * 4)
                for j in range(SUB):
                    mm = nc.tensor.transpose(UB[:, j * P:(j + 1) * P], tok[:, j, :], ident)
                mm.then_inc(hT_mm, 1)
                pe.wait_ge(hT_ready, i + 1)
                for j in range(SUB):
                    if j >= 2:
                        pe.wait_ge(raw_ready, i * SUB + j - 1)
                    nc.tensor.matmul((GB, OB)[j % 2][:, 0:3 * D], hT[:, j * P:(j + 1) * P], w_qkv[:],
                                     start=True, stop=True).then_inc(qkv_mm, 1)
                pe.wait_ge(raw_ready, i * SUB + SUB)
                pe.wait_ge(hi_ready, i * 4 + 4)
                for b in range(4):
                    pe.wait_ge(lo_ready, i * 2 + b // 2 + 1)
                    if b >= 2:
                        pe.wait_ge(qk_copied, i * 4 + b - 1)
                    bank = (UB, OB)[b % 2][:].bitcast(F16)
                    for gg in (0, 1):
                        for j in range(SUB):
                            n = j * H + (2 * (b % 2) + gg) * G
                            mm = nc.tensor.transpose(
                                bank[:, gg * TB + j * P:gg * TB + (j + 1) * P],
                                split[:, b // 2, n:n + G, :, :].rearrange("p n s d -> p (n s d)"), id16[:])
                    mm.then_inc(qk_tr, 1)
            pe.wait_ge(qk_copied, 4 * NB)
            pe.wait_ge(vg_ready, NB)
            pe.wait_ge(in_down, 16)

            def scores(i, k):
                g, s = k // ST, k % ST
                if s == 0:
                    pe.wait_ge(q_staged[g], (i + 1) * 5 * 16)
                for j in range(G):
                    if j % 2 == 0:
                        wait(pe, sig_done, i * 2 * ROUNDS + 2 * k + j // 2 - 1)
                    mm = nc.tensor.matmul(S[:, j, :], kT[:, g, s * P:(s + 1) * P], q_pad[:, g, j, :], start=True, stop=True)
                    if j % 2 == 1:
                        mm.then_inc(score_mm, 1)

            def values(i, k):
                g, s = k // ST, k % ST
                if s == 0:
                    wait(pe, coll_ready, i * NG + g)
                for j in range(G):
                    if j % 2 == 0:
                        pe.wait_ge(sig_done, i * 2 * ROUNDS + 2 * k + j // 2 + 1)
                    mm = nc.tensor.matmul(AV[32 * j:32 * j + HD, :], vg[:, s, G * g + j, :], res[:, k % 2, j, :],
                                          start=s == 0, stop=s == ST - 1)
                mm.then_inc(av_mm, 1)

            def gate_rows(i, g, before):
                pe.wait_ge(*before)
                nc.tensor.matmul(GB[:], gm_a[:], qT[:, g, :], start=True, stop=False)
                nc.tensor.matmul(GB[:], gm_b[:], qT[:, g, :], start=False, stop=True).then_inc(gateb_mm, 1)

            def project(i):
                pe.wait_ge(coll_ready, i * NG)
                pe.wait_ge(gateb_copied, i * NG)
                for j in range(SUB):
                    for g in range(NG):
                        mm = nc.tensor.matmul(GB[:, j * D:(j + 1) * D], coll[:, g, j * P:(j + 1) * P], wo_sb[:, g, :],
                                              start=g == 0, stop=g == NG - 1)
                mm.then_inc(proj_mm, 1)

            def turn_tokens(i):
                pe.wait_ge(n2_ready, i)
                for j in range(SUB):
                    mm = nc.tensor.transpose(UB[:, j * P:(j + 1) * P], tok[:, j, :], ident)
                mm.then_inc(n2_mm, 1)

            def route(i):
                pe.wait_ge(xn_ready, i * 3)
                for j in range(SUB):
                    mm = nc.tensor.matmul(GB[:, j * E:(j + 1) * E], xnT[:, j * P:(j + 1) * P], rw_sb[:], start=True, stop=True)
                mm.then_inc(router_mm, 1)

            def turn_comb(i, gate_reader):
                pe.wait_ge(comb_ready, i)
                pe.wait_ge(*gate_reader)
                for j in range(SUB):
                    mm = nc.tensor.matmul(GB[0:E, j * P:(j + 1) * P], hot[:, 2, j, :], ident, start=True, stop=True)
                mm.then_inc(combT_mm, 1)

            def three_passes(bank, a):
                for n, (w, v) in enumerate(((gu_hi, xn_hi), (gu_hi, xn_lo), (gu_lo, xn_hi))):
                    mm = nc.tensor.matmul(bank[:], w[:, a:a + P], v[:], start=n == 0, stop=n == 2)
                return mm

            def gate_up(i, c, gate_reader):
                n = (i - 1) * NCH + c
                a, gap = (c // FC * 2 * F + c % FC * P, F) if c < E * FC else (E * 2 * F, P)
                pe.wait_ge(*gate_reader)
                three_passes(GB, a).then_inc(gate_mm, 1)
                if c >= 2:
                    hidden_out(i, c - 2)
                if c == 0:
                    pe.wait_ge(xn_ready, i * 3)
                else:
                    pe.wait_ge(prod_ready, n)
                three_passes(UB, a + gap).then_inc(up_mm, 1)

            def hidden_out(i, c):
                pe.wait_ge(hid_ready, (i - 1) * NCH + c + 1)
                if c % FC == 0:
                    pe.wait_ge(acc_ready, (i - 1) * (E + 1) + c // FC)
                nc.tensor.matmul(OB[:], down_sb[:, c, :], hid[c % 2], start=c % FC == 0,
                                 stop=c % FC == FC - 1 or c == NCH - 1).then_inc(down_mm, 1)

            def turn_out(i):
                pe.wait_ge(acc_ready, i * (E + 1))
                for j in range(SUB):
                    mm = nc.tensor.transpose(UB[:, j * P:(j + 1) * P], acc[:, j * P:(j + 1) * P], ident)
                mm.then_inc(fin_mm, 1)

            def extras(i, k, attention):
                g, s = k // ST, k % ST
                if k == 0:
                    project(i)
                if k == 4:
                    turn_tokens(i)
                if k == 5:
                    route(i)
            def chunk_at(i, k, gate_reader):
                for c in range(NCH):
                    if chunk_round(c) == k:
                        gate_up(i, c, gate_reader)
                        return gate_clipped, (i - 1) * NCH + c + 1
                return gate_reader

            def rounds(i, experts):
                reader = (diff_ready, i) if experts else (qk_copied, 4 * NB)
                for k in range(ROUNDS):
                    scores(i, k)
                    if experts:
                        extras(i, k, True)
                        reader = chunk_at(i, k, reader)
                        if k == COMB_ROUND:
                            turn_comb(i, reader)
                            reader = (combT_ready, i)
                        if k == chunk_round(NCH - 1) + 1:
                            hidden_out(i, NCH - 2)
                        if k == chunk_round(NCH - 1) + 2:
                            hidden_out(i, NCH - 1)
                        if k == ROUNDS - 1:
                            turn_out(i)
                    if k % ST == 9:
                        gate_rows(i, k // ST, reader)
                        reader = (gateb_copied, i * NG + k // ST + 1)
                    if k > 0:
                        values(i, k - 1)
                values(i, ROUNDS - 1)

            pe.wait_ge(setup, 8)
            rounds(0, False)
            pe.wait_ge(w_lo, NSPL)
            with pe.Fori(1, NB) as i:
                rounds(i, True)
            project(NB)
            turn_tokens(NB)
            route(NB)
            reader = (diff_ready, NB)
            for c in range(NCH):
                gate_up(NB, c, reader)
                reader = (gate_clipped, (NB - 1) * NCH + c + 1)
                if c == COMB_CHUNK:
                    turn_comb(NB, reader)
                    reader = (combT_ready, NB)
            hidden_out(NB, NCH - 2)
            hidden_out(NB, NCH - 1)
            turn_out(NB)

        @block.vector
        def _(dve):
            v = nc.vector
            v.memset(sig_bias[:], -SHARP * THRESH).then_inc(setup, 1)
            v.memset(AV[:], 0.0).then_inc(setup, 1)
            dve.wait_ge(in_w, 6 * 16)
            v.tensor_copy(lnb_all[:], col(V_LNB).to_broadcast([P, P])).then_inc(setup, 1)
            dve.wait_ge(bias_mm, 1)
            v.tensor_copy(b_qk[:], GB[:, 0:2 * D]).then_inc(setup, 1)
            v.tensor_scalar(w_qkv[:, 0:2 * D], w_qkv[:, 0:2 * D], col(V_LNW), None, ALU.mult).then_inc(setup, 1)
            v.tensor_copy(gq16[:, 0:1], col(V_GQ)).then_inc(setup, 1)
            dve.wait_ge(setup, 6)
            setup_n = Steps(dve, pro, 0)
            setup_n(v.tensor_tensor(gq_parts[:, 0:1], col(V_GQ), gq16[:, 0:1], ALU.subtract))
            setup_n(v.tensor_copy(gq16[:, 1:2], gq_parts[:, 0:1]))
            setup_n(v.tensor_tensor(gq_parts[:, 1:2], gq_parts[:, 0:1], gq16[:, 1:2], ALU.subtract))
            setup_n(v.tensor_copy(gq16[:, 2:3], gq_parts[:, 1:2]))
            setup_n(v.tensor_copy(gq_parts[:, 2:5], gq16[:, 0:3]))
            setup_n(v.tensor_scalar(gm_t[:], const_sb[:, C_MA:C_MA + P], gq_parts[:, 2:3], None, ALU.mult))
            v.scalar_tensor_tensor(out=gm_a[:], in0=const_sb[:, C_MB:C_MB + P], scalar=gq_parts[:, 3:4], in1=gm_t[:],
                                   op0=ALU.mult, op1=ALU.add).then_inc(setup, 1)
            v.tensor_scalar(gm_b[:], const_sb[:, C_MA:C_MA + P], gq_parts[:, 4:5], None, ALU.mult).then_inc(setup, 1)
            SETUP = setup_n.n
            dve.wait_ge(in_x, 16 * NB)
            s_var, s_r1, s_r2, s_t, s_v2 = (small[:, n, :] for n in range(5))

            def stats(link, src):
                for j in range(SUB):
                    ins = v.bn_stats(bst[:, j, :], src(j))
                    if j < SUB - 1:
                        link.count(ins)
                    else:
                        link(ins, alone=True)
                for j in range(SUB):
                    ins = v.bn_aggr(mv[:, j, :], bst[:, j, :])
                    if j < SUB - 1:
                        link.count(ins)
                    else:
                        link(ins)

            def twice(link):
                link(v.tensor_scalar(s_var, mv[:, :, 1], EPS, None, ALU.add))
                rsqrt(link, s_var, s_r1, s_t)
                link(v.tensor_tensor(s_t, s_r1, s_r1, ALU.mult))
                link(v.tensor_tensor(s_v2, s_t, mv[:, :, 1], ALU.mult))
                link(v.tensor_scalar(s_v2, s_v2, EPS, None, ALU.add))
                rsqrt(link, s_v2, s_r2, s_t)

            with dve.Fori(0, NB) as i:
                link = Steps(dve, pro, i * PRO_STEPS + SETUP)
                stats(link, lambda j: x_sb[:, bass.ds(i * SUB + j, 1), :].rearrange("p o d -> p (o d)"))
                twice(link)
                dve.wait_ge(hT_mm, i)
                for j in range(SUB):
                    v.tensor_scalar(tok[:, j, :], x_sb[:, bass.ds(i * SUB + j, 1), :].rearrange("p o d -> p (o d)"),
                                    mv[:, j, 0:1], s_r1[:, j:j + 1], ALU.subtract, ALU.mult).then_inc(h_ready, 1)
                for j in range(SUB):
                    dve.wait_ge(raw_ready, i * SUB + j + 1)
                    if j == 0:
                        dve.wait_ge(hi_ready, i * 4)
                    v.scalar_tensor_tensor(
                        out=qk[:, :, j * D:(j + 1) * D], in0=raw[:, j, 0:2 * D].rearrange("p (w n) -> p w n", w=2),
                        scalar=s_r2[:, j:j + 1], in1=b_qk[:].rearrange("p (w n) -> p w n", w=2),
                        op0=ALU.mult, op1=ALU.add).then_inc(qk_ready, 1)
                dve.wait_ge(qk_ready, i * SUB + SUB)
                dve.wait_ge(sq_ready, i + 1)
                ss = ssq[:].rearrange("p w n -> p (w n)")
                link(v.tensor_reduce(ss, sq, AX_X, ALU.add))
                link(v.tensor_scalar(ss, ss, NORM_EPS * NORM_EPS, None, ALU.max))
                rsqrt(link, ss, rn[:], rn_t[:])
                link(v.tensor_scalar(rn[:], rn[:], QK_SCALE, None, ALU.mult))
                both = qk.rearrange("p w n -> p (w n)").rearrange("p (n d) -> p n d", d=HD)
                v.tensor_tensor(both, both, rn[:].unsqueeze(2).to_broadcast([P, 2 * SUB * H, HD]), ALU.mult).then_inc(unit_ready, 1)
                dve.wait_ge(unit_ready, i + 1)
                unit_k = qk[:, 1, :].rearrange("p (n d) -> p n d", d=HD)
                unit_q = qk[:, 0, :].rearrange("p (n d) -> p n d", d=HD)
                gk = vec_sb[:, V_GK:V_GK + HD].unsqueeze(1).to_broadcast([P, SUB * H, HD])
                link(v.tensor_tensor(sq[:, 0:SUB * H, :], unit_k, gk, ALU.mult))
                link(v.tensor_reduce(gk_s[:], sq[:, 0:SUB * H, :], AX_X, ALU.add))
                link(v.tensor_scalar(gk_s[:], gk_s[:], 1.0 / QK_SCALE, None, ALU.mult))
                v.tensor_tensor(vg[:, bass.ds(i * SUB, SUB), :, :],
                                raw[:, :, 2 * D:3 * D].rearrange("p s (h d) -> p s h d", d=HD),
                                gk_s[:].rearrange("p (s h) -> p s h", s=SUB).unsqueeze(3).to_broadcast([P, SUB, H, HD]),
                                ALU.mult).then_inc(vg_ready, 1)
                dve.wait_ge(hi_ready, i * 4 + 4)
                for w, unit, los in ((0, unit_q, (1, 3)), (1, unit_k, (2, 3))):
                    link(v.tensor_tensor(split[:, w, :, los[0], :], unit, split[:, w, :, 0, :], ALU.subtract))
                    v.tensor_copy(split[:, w, :, los[1], :], split[:, w, :, los[0], :]).then_inc(lo_ready, 1)
                assert link.n == PRO_STEPS, link.n

            def collapse(i, g):
                dve.wait_ge(av_mm, i * ROUNDS + (g + 1) * ST)
                dve.wait_ge(gateb_copied, i * NG + g + 1)
                if g == 0:
                    wait(dve, proj_mm, i)
                v.tensor_tensor(coll[:, g, :], AV[:], gate_q[:], ALU.mult).then_inc(coll_ready, 1)

            def attention_out(i, link):
                wait(dve, out_saved, (i - 1) * 16)
                dve.wait_ge(proj_mm, i)
                bo = vec_sb[:, V_BO:V_BO + D].unsqueeze(1).to_broadcast([P, SUB, D])
                link(v.tensor_tensor(tok[:], GB[:].rearrange("p (s d) -> p s d", s=SUB), bo, ALU.add))
                stats(link, lambda j: tok[:, j, :])
                link(v.tensor_scalar(s_var, mv[:, :, 1], EPS, None, ALU.add))
                rsqrt(link, s_var, s_r1, s_t)
                for j in range(SUB):
                    link(v.tensor_scalar(tok[:, j, :], tok[:, j, :], mv[:, j, 0:1], s_r1[:, j:j + 1], ALU.subtract, ALU.mult))
                link(v.tensor_tensor(x1, tok[:], x_sb[:, bass.ds((i - 1) * SUB, SUB), :], ALU.add))
                stats(link, lambda j: x1[:, j, :])
                twice(link)
                link(v.tensor_tensor(s_r1, s_r1, s_r2, ALU.mult))
                for j in range(SUB):
                    ins = v.tensor_scalar(tok[:, j, :], x1[:, j, :], mv[:, j, 0:1], s_r1[:, j:j + 1], ALU.subtract, ALU.mult)
                    if j < SUB - 1:
                        link(ins)
                    else:
                        ins.then_inc(n2_ready, 1)

            def expert_in(i):
                dve.wait_ge(n2_mm, i)
                v.tensor_scalar(xnT, UB[:], col(V_GAM), col(V_BET), ALU.mult, ALU.add).then_inc(xn_ready, 1)
                dve.wait_ge(xn_ready, i * 3 - 2)
                v.tensor_copy(xn_hi[:], xnT).then_inc(xn_ready, 1)
                dve.wait_ge(xn_ready, i * 3 - 1)
                v.tensor_tensor(xn_lo[:], xnT, xn_hi[:].bitcast(F32), ALU.subtract).then_inc(xn_ready, 1)

            def choose(i, link):
                dve.wait_ge(router_mm, i)
                link(v.tensor_copy(logit[:], GB[:, 0:SUB * E].rearrange("p (s e) -> p s e", s=SUB)), alone=True)
                for j in range(SUB):
                    ins = v.max(top[:, j, :], logit[:, j, :])
                    if j < SUB - 1:
                        link.count(ins)
                    else:
                        link(ins)
                v.tensor_tensor(tdiff[:], top[:, :, 1], top[:, :, 0], ALU.subtract).then_inc(diff_ready, 1)
                for j in range(SUB):
                    ins = v.max_index(topi[:, j, :], top[:, j, :], logit[:, j, :])
                    if j < SUB - 1:
                        link.count(ins)
                    else:
                        link(ins)
                link(v.tensor_copy(topf[:], topi[:, :, 0:2]))
                for n in (0, 1):
                    link(v.tensor_tensor(hot[:, n], iota.unsqueeze(1).to_broadcast([P, SUB, E]),
                                         topf[:, :, n:n + 1].to_broadcast([P, SUB, E]), ALU.is_equal))

            def combine(i, link):
                dve.wait_ge(twt_ready, i * 2)
                for n in (0, 1):
                    link(v.tensor_tensor(hot[:, n], hot[:, n], twt[:, n, :].unsqueeze(2).to_broadcast([P, SUB, E]), ALU.mult))
                v.tensor_tensor(hot[:, 2], hot[:, 0], hot[:, 1], ALU.add).then_inc(comb_ready, 1)

            def keep_comb(i):
                dve.wait_ge(combT_mm, i)
                v.tensor_copy(combT, GB[0:E, :]).then_inc(combT_ready, 1)

            def hidden(i, c):
                n = (i - 1) * NCH + c
                dve.wait_ge(gate_mm, n + 1)
                if c >= 2:
                    dve.wait_ge(sg_ready, n - 1)
                v.tensor_scalar(gate_c[c % 2], GB[:], 10.0, -10.0, ALU.min, ALU.max).then_inc(gate_clipped, 1)
                dve.wait_ge(up_mm, n + 1)
                dve.wait_ge(gate_clipped, n + 1)
                if c >= 2:
                    dve.wait_ge(hid_ready, n - 1)
                v.tensor_tensor(prod[c % 2], gate_c[c % 2], UB[:], ALU.mult).then_inc(prod_ready, 1)

            def add_expert(i, e, link):
                n = (i - 1) * (E + 1)
                dve.wait_ge(down_mm, (i - 1) * NCH + min((e + 1) * FC, NCH))
                if e < E:
                    dve.wait_ge(comb_in[e % 2], ((i - 1) * (E // 2) + e // 2 + 1) * 16)
                if e == 0:
                    v.tensor_tensor(acc, OB[:], comb_all[:, 0, :], ALU.mult).then_inc(acc_ready, 1)
                elif e < E:
                    link(v.tensor_tensor(tmp, OB[:], comb_all[:, e % 2, :], ALU.mult))
                    dve.wait_ge(acc_ready, n + e)
                    v.tensor_tensor(acc, acc, tmp, ALU.add).then_inc(acc_ready, 1)
                else:
                    dve.wait_ge(acc_ready, n + e)
                    v.tensor_tensor(acc, acc, OB[:], ALU.add).then_inc(acc_ready, 1)

            def finish(i, link):
                dve.wait_ge(fin_mm, i)
                stats(link, lambda j: UB[:, j * P:(j + 1) * P])
                link(v.tensor_scalar(s_var, mv[:, :, 1], EPS, None, ALU.add))
                rsqrt(link, s_var, s_r1, s_t)
                for j in range(SUB):
                    v.tensor_scalar(tok[:, j, :], UB[:, j * P:(j + 1) * P], mv[:, j, 0:1], s_r1[:, j:j + 1],
                                    ALU.subtract, ALU.mult).then_inc(fin_read, 1)
                dve.wait_ge(fin_read, i * SUB)
                v.tensor_tensor(tok[:], tok[:], x1, ALU.add).then_inc(out_ready, 1)

            def rounds(i, experts):
                link = Steps(dve, blk, (i - 1) * BLK_STEPS) if experts else None
                for k in range(ROUNDS):
                    if experts:
                        if k == 0:
                            attention_out(i, link)
                        if k == 5:
                            expert_in(i)
                        if k == 6:
                            choose(i, link)
                            combine(i, link)
                        for c in range(NCH):
                            if chunk_round(c) == k:
                                hidden(i, c)
                                if c == COMB_CHUNK:
                                    keep_comb(i)
                                if c >= 5 and c % FC == 1:
                                    add_expert(i, c // FC - 1, link)
                        if k == chunk_round(NCH - 1) + 1:
                            add_expert(i, E - 1, link)
                        if k == chunk_round(NCH - 1) + 2:
                            add_expert(i, E, link)
                    if k % ST == 0 and k > 0:
                        collapse(i, k // ST - 1)
                collapse(i, NG - 1)
                if experts:
                    finish(i, link)
                    assert link.n == BLK_STEPS, link.n

            rounds(0, False)
            with dve.Fori(1, NB) as i:
                rounds(i, True)
            link = Steps(dve, blk, (NB - 1) * BLK_STEPS)
            attention_out(NB, link)
            expert_in(NB)
            choose(NB, link)
            combine(NB, link)
            for c in range(NCH):
                hidden(NB, c)
                if c == COMB_CHUNK:
                    keep_comb(NB)
                if c >= 5 and c % FC == 1:
                    add_expert(NB, c // FC - 1, link)
            add_expert(NB, E - 1, link)
            add_expert(NB, E, link)
            finish(NB, link)


def _layout(inputs):
    import numpy as np

    a = {k[3:]: np.asarray(v) for k, v in inputs.items()}
    f = np.float32
    rows = np.arange(P)
    same_head = rows[:, None] // 32 == rows[None, :] // 32
    first = (rows[:, None] % 32) < 16
    consts = np.concatenate([np.eye(P), same_head & first, same_head & ~first,
                             np.broadcast_to(np.arange(E), (P, E))], axis=1).astype(f)
    gq = np.tile(a["attn_gq"], P // HD)[:, None]
    gk = np.broadcast_to(a["attn_gk"], (P, HD))
    bo = np.broadcast_to(a["attn_bo"], (P, D))
    vecs = np.concatenate([a["attn_ln_w"][:, None], a["attn_ln_b"][:, None], a["ffn_ln_gamma"][:, None],
                           a["ffn_ln_beta"][:, None], gq, gk, bo], axis=1)
    wo = np.zeros((G, 32, NG, D), f)
    wo[:, :HD] = a["attn_Wo"].reshape(NG, G, HD, D).transpose(1, 2, 0, 3)
    gu = np.concatenate([a["ffn_gate_up_w"].transpose(1, 0, 2).reshape(D, E * 2 * F), a["ffn_shared_gate_up_w"]], axis=1)
    down = np.concatenate([a["ffn_down_w"].reshape(E * FC, P, D), a["ffn_shared_down_w"][None]]).transpose(1, 0, 2)
    return {
        "x": a["attn_x"].reshape(ST, P, D).transpose(1, 0, 2),
        "wqkv": np.concatenate([a["attn_Wq"], a["attn_Wk"], a["attn_Wv"]], axis=1),
        "vecs": vecs, "consts": consts, "ident16": np.eye(P, dtype=np.float16),
        "wo": wo.reshape(P, NG, D), "router": a["ffn_router_w"], "gu": gu, "down": down,
    }


def kernel(**inputs):
    import numpy as _np
    import concourse.bacc as _bacc
    from concourse import mybir as _mybir
    from concourse.bass_utils import run_bass_kernel_spmd as _run

    nc = _bacc.Bacc("TRN2", target_bir_lowering=False, num_devices=1)
    arrays, args = {}, []
    for name, a in _layout(inputs).items():
        a = _np.ascontiguousarray(a)
        arrays[f"in_{name}"] = a
        args.append(nc.dram_tensor(f"in_{name}", a.shape, _mybir.dt.from_np(a.dtype), kind="ExternalInput").ap())
    args.append(nc.dram_tensor("out_0", (P, ST, D), _mybir.dt.float32, kind="ExternalOutput").ap())
    build(nc, *args)
    r = _run(nc, [arrays], core_ids=[0])
    got = r.results[0]["out_0"]
    return got.transpose(1, 0, 2).reshape(1, T, D)
```

```python
from contextlib import ExitStack

import concourse.bass as bass
from concourse import mybir

P = 128
T = 2048
D = 128
H = 16
HD = D // H
SLOTS = 4
G = 4
NG = H // G
TB = 512
SUB = TB // P
NB = T // TB
ST = T // P
E = 8
F = 512
FC = F // P
NCH = E * FC + 1
GU = E * 2 * F + 2 * P
ROUNDS = NG * ST
SPL = 1024
NSPL = -(-GU // SPL)

THRESH, SHARP, EPS, NORM_EPS = 0.29514, 15.0, 1e-5, 1e-12
QK_SCALE = 64.0
RSQRT_MAGIC = 1597463007.0

F32 = mybir.dt.float32
F32R = mybir.dt.float32r
F16 = mybir.dt.float16
BF16 = mybir.dt.bfloat16
I32 = mybir.dt.int32
U32 = mybir.dt.uint32
ALU = mybir.AluOpType
ACT = mybir.ActivationFunctionType
AX_X = mybir.AxisListType.X

C_ID, C_MA, C_MB, C_IO = 0, P, 2 * P, 3 * P
V_LNW, V_LNB, V_GAM, V_BET, V_GQ, V_GK, V_BO = 0, 1, 2, 3, 4, 5, 5 + HD
NCONST, NVEC = 3 * P + E, 5 + HD + D

BLK_STEPS = 90


TURN_ROUND, ROUTE_ROUND, FIRST_UNIT, LAST_UNIT = 8, 9, 10, 61
PROLOGUE = [("project", 0), ("square", 0), ("project", 1), ("high", 0),
            ("square", 1), ("turn", 0), ("high", 1), ("project", 2), ("rounds", 2),
            ("square", 2), ("turn", 1), ("rounds", 1), ("high", 2), ("project", 3), ("rounds", 2),
            ("square", 3), ("turn", 2), ("rounds", 1), ("high", 3), ("rounds", 2), ("turn", 3)]
COMB_CHUNK = 1


def unit_round(c, part):
    return FIRST_UNIT + (3 * c + part) * (LAST_UNIT - FIRST_UNIT) // (3 * (NCH + 1))


def build(nc, x, wqkv, vecs, consts, ident16, wo, router, gu, down, out):
    ctx = ExitStack()
    with ctx:
        def sb(name, shape, dt=F32):
            return ctx.enter_context(nc.sbuf_tensor(name, shape, dt))

        def sem(name):
            return ctx.enter_context(nc.semaphore(name))

        x_sb = sb("x_sb", [P, ST, D])
        const_sb = sb("const_sb", [P, NCONST])
        vec_sb = sb("vec_sb", [P, NVEC])
        id16 = sb("id16", [P, P], F16)
        w_qkv = sb("w_qkv", [P, 3 * D])
        wo_sb = sb("wo_sb", [P, NG, D])
        rw_sb = sb("rw_sb", [P, E])
        lnb_all = sb("lnb_all", [P, P])
        b_qk = sb("b_qk", [P, 2 * D])
        gu_hi = sb("gu_hi", [P, GU], F32R)
        gu_lo = sb("gu_lo", [P, GU], F32R)
        down_sb = sb("down_sb", [P, NCH, D])
        vg = sb("vg", [P, ST, H, HD])
        kT = sb("kT", [P, NG, T], F16)
        qT = sb("qT", [P, NG, TB], F16)
        q_pad = sb("q_pad", [P, NG, G, TB], F16)
        res = sb("res", [P, 2, G, TB])
        coll = sb("coll", [P, NG, TB])
        gate_q = sb("gate_q", [P, TB])
        gq_parts = sb("gq_parts", [P, 8])
        gq16 = sb("gq16", [P, 3], BF16)
        gm_a = sb("gm_a", [P, P], BF16)
        gm_b = sb("gm_b", [P, P], BF16)
        gm_t = sb("gm_t", [P, P])
        sig_bias = sb("sig_bias", [P, 1])
        tok = sb("tok", [P, SUB, D])
        xn_hi = sb("xn_hi", [P, TB], F32R)
        xn_lo = sb("xn_lo", [P, TB], F32R)
        comb_all = sb("comb_all", [P, 2, TB])
        bst = sb("bst", [P, ST - SUB, 6])
        mv = sb("mv", [P, ST, 2])
        small = sb("small", [P, 3, SUB])
        var12 = sb("var12", [P, 2, ST])
        fac12 = sb("fac12", [P, 2, ST])
        fac_t = sb("fac_t", [P, 2, ST])
        fac2 = sb("fac2", [P, ST])
        logit = sb("logit", [P, SUB, E])
        top = sb("top", [P, SUB, 8])
        topi = sb("topi", [P, SUB, 8], U32)
        topf = sb("topf", [P, SUB, 2])
        pause = sb("pause", [P, 1])
        tdiff = sb("tdiff", [P, SUB])
        twt = sb("twt", [P, 2, SUB])
        hot = sb("hot", [P, 3, SUB, E])
        work = sb("work", [P, 12 * TB])
        gate_c = [work[:, n * TB:(n + 1) * TB] for n in (0, 1)]
        prod = [work[:, n * TB:(n + 1) * TB] for n in (2, 3)]
        sg = [work[:, n * TB:(n + 1) * TB] for n in (4, 5)]
        hid = [work[:, n * TB:(n + 1) * TB] for n in (6, 7)]
        x1 = work[:, 8 * TB:9 * TB].rearrange("p (s d) -> p s d", s=SUB)
        acc = work[:, 9 * TB:10 * TB]
        tmp = work[:, 10 * TB:11 * TB]
        xnT = work[:, 11 * TB:12 * TB]
        combT = tmp[0:E, :]
        raw_w = [work[:, n * SPL:(n + 1) * SPL] for n in (0, 1)]
        hT = work[:, 0:TB]
        raw = [m.rearrange("p (s n) -> p s n", s=SUB)
               for m in (work[:, TB:4 * TB], coll[:, 0:3, :].rearrange("p g t -> p (g t)"))]
        q_out = comb_all[:].rearrange("p n t -> p (n t)").bitcast(F16).rearrange("p (g t) -> p g t", g=NG)
        qk = work[:, 4 * TB:6 * TB].rearrange("p (w n) -> p w n", w=2)
        sq = work[:, 6 * TB:8 * TB].rearrange("p (n d) -> p n d", d=HD)
        split = work[:, 8 * TB:12 * TB].bitcast(F16).rearrange(
            "p (w n s d) -> p w n s d", w=2, s=SLOTS, d=HD)
        ssq = sb("ssq", [P, 2, SUB * H])
        rn = sb("rn", [P, 2 * SUB * H])
        rn_t = sb("rn_t", [P, 2 * SUB * H])
        gk_s = sb("gk_s", [P, SUB * H])

        q_dram = nc.dram_tensor("q_dram", (NB, P, NG, TB), F16).ap()
        comb_dram = nc.dram_tensor("comb_dram", (E, TB), F32).ap()

        S = ctx.enter_context(nc.psum_tensor("S", [P, G, TB], F32))
        AV = ctx.enter_context(nc.psum_tensor("AV", [P, TB], F32))
        GB = ctx.enter_context(nc.psum_tensor("GB", [P, TB], F32))
        UB = ctx.enter_context(nc.psum_tensor("UB", [P, TB], F32))
        OB = ctx.enter_context(nc.psum_tensor("OB", [P, TB], F32))

        ident = const_sb[:, C_ID:C_ID + P]
        iota = const_sb[:, C_IO:C_IO + E]

        def col(n):
            return vec_sb[:, n:n + 1]

        in_x = sem("in_x")
        in_xs = sem("in_xs")
        in_w = sem("in_w")
        in_down = sem("in_down")
        in_raw = [sem("in_raw0"), sem("in_raw1")]
        zeroed = sem("zeroed")
        setup = sem("setup")
        bias_mm = sem("bias_mm")
        pro = sem("pro")
        h_ready = sem("h_ready")
        hT_mm = sem("hT_mm")
        hT_ready = sem("hT_ready")
        qkv_mm = sem("qkv_mm")
        raw_ready = sem("raw_ready")
        qk_ready = sem("qk_ready")
        sq_ready = sem("sq_ready")
        unit_ready = sem("unit_ready")
        hi_ready = sem("hi_ready")
        lo_ready = sem("lo_ready")
        vg_ready = sem("vg_ready")
        qk_tr = sem("qk_tr")
        qk_copied = sem("qk_copied")
        q_saved = sem("q_saved")
        q0_staged = sem("q0_staged")
        act_warm = sem("act_warm")
        q_staged = [sem(f"q_staged{g}") for g in range(NG)]
        w_hi = sem("w_hi")
        w_lo = sem("w_lo")
        score_mm = sem("score_mm")
        sig_done = sem("sig_done")
        av_mm = sem("av_mm")
        gateb_mm = sem("gateb_mm")
        gateb_copied = sem("gateb_copied")
        coll_ready = sem("coll_ready")
        proj_mm = sem("proj_mm")
        blk = sem("blk")
        n2_ready = sem("n2_ready")
        n2_mm = sem("n2_mm")
        xn_ready = sem("xn_ready")
        router_mm = sem("router_mm")
        diff_ready = sem("diff_ready")
        twt_ready = sem("twt_ready")
        comb_ready = sem("comb_ready")
        combT_mm = sem("combT_mm")
        combT_ready = sem("combT_ready")
        comb_saved = sem("comb_saved")
        comb_in = [sem("comb_in0"), sem("comb_in1")]
        gate_mm = sem("gate_mm")
        up_mm = sem("up_mm")
        gate_clipped = sem("gate_clipped")
        prod_ready = sem("prod_ready")
        sg_ready = sem("sg_ready")
        hid_ready = sem("hid_ready")
        down_mm = sem("down_mm")
        acc_ready = sem("acc_ready")
        fin_mm = sem("fin_mm")
        fin_read = sem("fin_read")
        out_ready = sem("out_ready")
        out_saved = sem("out_saved")

        def rsqrt(link, v, y, t):
            link(nc.vector.tensor_scalar(t.bitcast(I32), v.bitcast(I32), 1, None, ALU.logical_shift_right))
            link(nc.vector.tensor_scalar(y.bitcast(I32), t.bitcast(I32), -1.0, RSQRT_MAGIC, ALU.mult, ALU.add))
            for _ in range(3):
                link(nc.vector.scalar_tensor_tensor(out=t, in0=y, scalar=-0.5, in1=y, op0=ALU.mult, op1=ALU.mult))
                link(nc.vector.tensor_tensor(t, t, v, ALU.mult))
                link(nc.vector.scalar_tensor_tensor(out=y, in0=t, scalar=1.5, in1=y, op0=ALU.add, op1=ALU.mult))

        class Steps:

            def __init__(self, eng, s, base):
                self.eng, self.s, self.base, self.n = eng, s, base, 0

            def count(self, ins):
                self.n += 1
                ins.then_inc(self.s, 1)

            def __call__(self, ins, alone=False):
                self.count(ins)
                self.eng.wait_ge(self.s, self.base + self.n)
                if alone:
                    self.eng.memset(pause[:], 0.0)

        def wait(eng, s, value):
            if not isinstance(value, int) or value > 0:
                eng.wait_ge(s, value)

        block = ctx.enter_context(nc.Block())

        @block.sync
        def _(sp):
            sp.dma_start(x_sb[:, 0:SUB, :], x[:, 0:SUB, :]).then_inc(in_x, 16)
            for dst, src in ((w_qkv, wqkv), (wo_sb, wo), (rw_sb, router)):
                sp.dma_start(dst[:], src).then_inc(in_w, 16)
            sp.dma_start(x_sb[:, SUB:ST, :], x[:, SUB:ST, :]).then_inc(in_xs, 16)
            sp.dma_start(down_sb[:], down).then_inc(in_down, 16)
            sp.wait_ge(zeroed, 1)
            sp.wait_ge(qk_copied, 2)
            for j in range(G):
                r = slice(32 * j, 32 * j + 32)
                sp.dma_start(q_pad[r, :, j, :], qT[r, :, :]).then_inc(q0_staged, 16)
            for b in range(NB):
                sp.wait_ge(qk_copied, 4 * b + 2)
                sp.dma_start(q_dram[b], q_out if b else qT[:]).then_inc(q_saved, 16)
            sp.wait_ge(qk_copied, 4 * NB)
            sp.wait_ge(vg_ready, NB)
            for n in range(NSPL):
                w = min(SPL, GU - n * SPL)
                if n >= 2:
                    sp.wait_ge(w_lo, n - 1)
                sp.dma_start(raw_w[n % 2][:, 0:w], gu[:, n * SPL:n * SPL + w]).then_inc(in_raw[n % 2], 16)

            def stage(i, g, nxt):
                sp.wait_ge(gateb_mm, i * NG + g + 1)
                if isinstance(nxt, int):
                    src = q_dram[nxt]
                else:
                    src = q_dram[bass.ds(nxt, 1)].rearrange("o p g t -> (o p) g t")
                for j in range(G):
                    r = slice(32 * j, 32 * j + 32)
                    sp.dma_start(q_pad[r, g, j, :], src[r, g, :]).then_inc(q_staged[g], 16)
                sp.dma_start(qT[:, g, :], src[:, g, :]).then_inc(q_staged[g], 16)

            def experts(i, attention):
                nxt = sp.snap((i + 1) % NB) if attention else None
                sp.wait_ge(combT_ready, i)
                sp.dma_start(comb_dram, combT).then_inc(comb_saved, 16)
                sp.wait_ge(comb_saved, i * 16)
                staged = 0
                for e in range(E):
                    while attention and e >= 2 and (staged + 1) * ST < unit_round(FC * (e - 1) + 1, 1):
                        stage(i, staged, nxt)
                        staged += 1
                    if e >= 2:
                        sp.wait_ge(acc_ready, (i - 1) * (E + 1) + e - 1)
                    sp.dma_start(comb_all[:, e % 2, :], comb_dram[e, :].partition_broadcast(P)).then_inc(comb_in[e % 2], 16)
                for g in range(staged, NG if attention else 0):
                    stage(i, g, nxt)
                sp.wait_ge(out_ready, i)
                sp.dma_start(out[:, bass.ds((i - 1) * SUB, SUB), :], tok[:]).then_inc(out_saved, 16)

            sp.wait_ge(q_saved, 16 * NB)
            for g in range(NG):
                stage(0, g, 1)
            with sp.Fori(1, NB) as i:
                experts(i, True)
            experts(NB, False)
            sp.wait_ge(out_saved, 16 * NB)
            for g in range(NG):
                sp.wait_ge(q_staged[g], NB * 5 * 16)

        @block.gpsimd
        def _(pool):
            nc.gpsimd.memset(q_pad[:].rearrange("p g j t -> p (g j t)").bitcast(F32), 0.0).then_inc(zeroed, 1)
            for n in range(NSPL):
                a, w = n * SPL, min(SPL, GU - n * SPL)
                pool.wait_ge(in_raw[n % 2], 16 * (n // 2 + 1))
                nc.gpsimd.tensor_scalar(gu_hi[:, a:a + w], raw_w[n % 2][:, 0:w], 1.0, 0.0, ALU.mult, ALU.add).then_inc(w_hi, 1)
                pool.wait_ge(w_hi, n + 1)
                nc.gpsimd.tensor_tensor(gu_lo[:, a:a + w], raw_w[n % 2][:, 0:w], gu_hi[:, a:a + w].bitcast(F32),
                                        ALU.subtract).then_inc(w_lo, 1)

            def experts(i):
                for c in range(NCH):
                    n = (i - 1) * NCH + c
                    pool.wait_ge(prod_ready, n + 1)
                    pool.wait_ge(sg_ready, n + 1)
                    if c >= 2:
                        pool.wait_ge(down_mm, n - 1)
                    nc.gpsimd.tensor_tensor(hid[c % 2], prod[c % 2], sg[c % 2], ALU.mult).then_inc(hid_ready, 1)

            with pool.Fori(1, NB) as i:
                experts(i)
            experts(NB)

        @block.scalar
        def _(act):
            for dst, src in ((const_sb, consts), (vec_sb, vecs), (id16, ident16)):
                act.dma_start(dst[:], src).then_inc(in_w, 16)
            act.wait_ge(setup, 1)
            nc.scalar.activation(twt[:, 0, 0:1], sig_bias[:], ACT.Sigmoid).then_inc(act_warm, 1)

            def project(b):
                act.wait_ge(hT_mm, b + 1)
                nc.scalar.activation(hT, UB[:], ACT.Copy).then_inc(hT_ready, 1)
                if b >= 2:
                    act.wait_ge(vg_ready, b - 1)
                for j in range(SUB):
                    act.wait_ge(qkv_mm, b * SUB + j + 1)
                    nc.scalar.activation(raw[b % 2][:, j, :], (GB, OB)[j % 2][:, 0:3 * D], ACT.Copy).then_inc(raw_ready, 1)

            def square(b):
                act.wait_ge(qk_ready, b * SUB + SUB)
                nc.scalar.activation(sq, qk.rearrange("p w n -> p (w n)").rearrange("p (n d) -> p n d", d=HD),
                                     ACT.Square).then_inc(sq_ready, 1)

            def high_parts(b):
                act.wait_ge(unit_ready, b + 1)
                for w, slots in ((0, (0, 2)), (1, (0, 1))):
                    for s in slots:
                        nc.scalar.activation(split[:, w, :, s, :], qk[:, w, :].rearrange("p (n d) -> p n d", d=HD),
                                             ACT.Copy).then_inc(hi_ready, 1)

            def turn(b):
                for n in range(4):
                    dst = (q_out if b else qT[:]) if n < 2 else kT[:, :, b * TB:(b + 1) * TB]
                    g = 2 * (n % 2)
                    if n == 0 and b >= 2:
                        act.wait_ge(q_saved, b * 16)
                    act.wait_ge(qk_tr, b * 4 + n + 1)
                    nc.scalar.activation(dst[:, g:g + 2, :], (UB, OB)[n % 2][:].bitcast(F16).rearrange("p (g t) -> p g t", g=2),
                                         ACT.Copy).then_inc(qk_copied, 1)

            def silu(i, c):
                n = (i - 1) * NCH + c
                act.wait_ge(gate_clipped, n + 1)
                if c >= 2:
                    act.wait_ge(hid_ready, n - 1)
                nc.scalar.activation(sg[c % 2], gate_c[c % 2], ACT.Sigmoid).then_inc(sg_ready, 1)

            def top_weights(i):
                act.wait_ge(diff_ready, i)
                nc.scalar.activation(twt[:, 0, :], tdiff[:], ACT.Sigmoid, scale=-1.0).then_inc(twt_ready, 1)
                nc.scalar.activation(twt[:, 1, :], tdiff[:], ACT.Sigmoid).then_inc(twt_ready, 1)

            def sigmoids(i, k):
                for half in (0, 1):
                    act.wait_ge(score_mm, i * 2 * ROUNDS + 2 * k + half + 1)
                    if half == 0:
                        wait(act, av_mm, i * ROUNDS + k - 1)
                    nc.scalar.activation(
                        res[:, k % 2, 2 * half:2 * half + 2, :].rearrange("p h t -> p (h t)"),
                        S[:, 2 * half:2 * half + 2, :].rearrange("p h t -> p (h t)"), ACT.Sigmoid,
                        bias=-SHARP * THRESH, scale=SHARP / (QK_SCALE * QK_SCALE)).then_inc(sig_done, 1)

            def rounds(i, experts, first=0):
                for k in range(first, ROUNDS):
                    sigmoids(i, k)
                    if experts:
                        if k == ROUTE_ROUND:
                            top_weights(i)
                        for c in range(NCH):
                            if unit_round(c, 0) == k:
                                silu(i, c)

            done = 0
            for what, b in PROLOGUE:
                if what == "rounds":
                    for k in range(done, done + b):
                        sigmoids(0, k)
                    done += b
                else:
                    {"project": project, "square": square, "high": high_parts, "turn": turn}[what](b)
            rounds(0, False, done)
            with act.Fori(1, NB) as i:
                rounds(i, True)
            top_weights(NB)
            for c in range(NCH):
                silu(NB, c)

        @block.tensor
        def _(pe):
            pe.wait_ge(in_w, 6 * 16)
            pe.wait_ge(setup, 3)
            nc.tensor.matmul(GB[:, 0:2 * D], lnb_all[:], w_qkv[:, 0:2 * D], start=True, stop=True).then_inc(bias_mm, 1)
            def project_qkv(b):
                pe.wait_ge(h_ready, b * SUB + SUB)
                wait(pe, qk_copied, 4 * (b - 1))
                for j in range(SUB):
                    mm = nc.tensor.transpose(UB[:, j * P:(j + 1) * P], tok[:, j, :], ident)
                mm.then_inc(hT_mm, 1)
                pe.wait_ge(hT_ready, b + 1)
                if b == 0:
                    pe.wait_ge(setup, 5)
                for j in range(SUB):
                    if j >= 2:
                        pe.wait_ge(raw_ready, b * SUB + j - 1)
                    nc.tensor.matmul((GB, OB)[j % 2][:, 0:3 * D], hT[:, j * P:(j + 1) * P], w_qkv[:],
                                     start=True, stop=True).then_inc(qkv_mm, 1)

            def turn_qk(b, projected):
                pe.wait_ge(raw_ready, projected * SUB)
                pe.wait_ge(hi_ready, b * 4 + 4)
                for n in range(4):
                    pe.wait_ge(lo_ready, b * 2 + n // 2 + 1)
                    if n >= 2:
                        pe.wait_ge(qk_copied, b * 4 + n - 1)
                    bank = (UB, OB)[n % 2][:].bitcast(F16)
                    for gg in (0, 1):
                        for j in range(SUB):
                            first = j * H + (2 * (n % 2) + gg) * G
                            mm = nc.tensor.transpose(
                                bank[:, gg * TB + j * P:gg * TB + (j + 1) * P],
                                split[:, n // 2, first:first + G, :, :].rearrange("p n s d -> p (n s d)"), id16[:])
                    mm.then_inc(qk_tr, 1)

            def scores(i, k):
                g, s = k // ST, k % ST
                if isinstance(i, int) and i == 0:
                    pe.wait_ge(qk_copied, 4 * (s // SUB + 1))
                    pe.wait_ge(q0_staged, 16 * G)
                elif s == 0:
                    pe.wait_ge(q_staged[g], i * 5 * 16)
                for j in range(G):
                    if j % 2 == 0:
                        wait(pe, sig_done, i * 2 * ROUNDS + 2 * k + j // 2 - 1)
                    mm = nc.tensor.matmul(S[:, j, :], kT[:, g, s * P:(s + 1) * P], q_pad[:, g, j, :], start=True, stop=True)
                    if j % 2 == 1:
                        mm.then_inc(score_mm, 1)

            def values(i, k):
                g, s = k // ST, k % ST
                if s == 0:
                    wait(pe, coll_ready, i * NG + g)
                if isinstance(i, int) and i == 0:
                    pe.wait_ge(vg_ready, s // SUB + 1)
                for j in range(G):
                    if j % 2 == 0:
                        pe.wait_ge(sig_done, i * 2 * ROUNDS + 2 * k + j // 2 + 1)
                    mm = nc.tensor.matmul(AV[32 * j:32 * j + HD, :], vg[:, s, G * g + j, :], res[:, k % 2, j, :],
                                          start=s == 0, stop=s == ST - 1)
                mm.then_inc(av_mm, 1)

            def gate_rows(i, g, before):
                pe.wait_ge(*before)
                if isinstance(i, int) and g == 0:
                    pe.wait_ge(setup, 8)
                nc.tensor.matmul(GB[:], gm_a[:], qT[:, g, :], start=True, stop=False)
                nc.tensor.matmul(GB[:], gm_b[:], qT[:, g, :], start=False, stop=True).then_inc(gateb_mm, 1)

            def project(i):
                pe.wait_ge(coll_ready, i * NG)
                pe.wait_ge(gateb_copied, i * NG)
                for j in range(SUB):
                    for g in range(NG):
                        mm = nc.tensor.matmul(GB[:, j * D:(j + 1) * D], coll[:, g, j * P:(j + 1) * P], wo_sb[:, g, :],
                                              start=g == 0, stop=g == NG - 1)
                mm.then_inc(proj_mm, 1)

            def turn_tokens(i):
                pe.wait_ge(n2_ready, i)
                for j in range(SUB):
                    mm = nc.tensor.transpose(UB[:, j * P:(j + 1) * P], tok[:, j, :], ident)
                mm.then_inc(n2_mm, 1)

            def route(i):
                pe.wait_ge(xn_ready, i * 3)
                for j in range(SUB):
                    mm = nc.tensor.matmul(GB[:, j * E:(j + 1) * E], xnT[:, j * P:(j + 1) * P], rw_sb[:], start=True, stop=True)
                mm.then_inc(router_mm, 1)

            def turn_comb(i, gate_reader):
                pe.wait_ge(comb_ready, i)
                pe.wait_ge(*gate_reader)
                for j in range(SUB):
                    mm = nc.tensor.matmul(GB[0:E, j * P:(j + 1) * P], hot[:, 2, j, :], ident, start=True, stop=True)
                mm.then_inc(combT_mm, 1)

            def three_passes(bank, a):
                for n, (w, v) in enumerate(((gu_hi, xn_hi), (gu_hi, xn_lo), (gu_lo, xn_hi))):
                    mm = nc.tensor.matmul(bank[:], w[:, a:a + P], v[:], start=n == 0, stop=n == 2)
                return mm

            def gate_up(i, c, part, gate_reader):
                n = (i - 1) * NCH + c
                a, gap = (c // FC * 2 * F + c % FC * P, F) if c < E * FC else (E * 2 * F, P)
                if part == 0:
                    pe.wait_ge(*gate_reader)
                    three_passes(GB, a).then_inc(gate_mm, 1)
                    return gate_clipped, n + 1
                if part == 1:
                    if c >= 2:
                        hidden_out(i, c - 2)
                    return gate_reader
                if c == 0:
                    pe.wait_ge(xn_ready, i * 3)
                else:
                    pe.wait_ge(prod_ready, n)
                three_passes(UB, a + gap).then_inc(up_mm, 1)
                if c == COMB_CHUNK:
                    turn_comb(i, gate_reader)
                    return combT_ready, i
                return gate_reader

            def hidden_out(i, c):
                pe.wait_ge(hid_ready, (i - 1) * NCH + c + 1)
                if c % FC == 0 and c > 0:
                    pe.wait_ge(acc_ready, (i - 1) * (E + 1) + c // FC)
                nc.tensor.matmul(OB[:], down_sb[:, c, :], hid[c % 2], start=c % FC == 0,
                                 stop=c % FC == FC - 1 or c == NCH - 1).then_inc(down_mm, 1)

            def turn_out(i):
                pe.wait_ge(acc_ready, i * (E + 1))
                for j in range(SUB):
                    mm = nc.tensor.transpose(UB[:, j * P:(j + 1) * P], acc[:, j * P:(j + 1) * P], ident)
                mm.then_inc(fin_mm, 1)

            def rounds(i, experts, first=0):
                reader = (diff_ready, i) if experts else (qk_copied, 4 * NB)
                for k in range(first, ROUNDS):
                    scores(i, k)
                    if experts:
                        if k == 0:
                            project(i)
                        if k == TURN_ROUND:
                            turn_tokens(i)
                        if k == ROUTE_ROUND:
                            route(i)
                        for c in range(NCH):
                            for part in range(3):
                                if unit_round(c, part) == k:
                                    reader = gate_up(i, c, part, reader)
                        if k == unit_round(NCH, 0):
                            hidden_out(i, NCH - 2)
                        if k == LAST_UNIT + 1:
                            hidden_out(i, NCH - 1)
                        if k == ROUNDS - 1:
                            turn_out(i)
                    if k % ST == ST - 1:
                        gate_rows(i, k // ST, reader)
                        reader = (gateb_copied, i * NG + k // ST + 1)
                    if k > 0:
                        values(i, k - 1)
                values(i, ROUNDS - 1)

            done, projected = 0, 0
            for what, b in PROLOGUE:
                if what == "project":
                    project_qkv(b)
                    projected += 1
                elif what == "turn":
                    turn_qk(b, projected)
                elif what == "rounds":
                    for k in range(done, done + b):
                        scores(0, k)
                        if k > 0:
                            values(0, k - 1)
                    done += b
            rounds(0, False, done)
            pe.wait_ge(in_down, 16)
            pe.wait_ge(w_lo, NSPL)
            with pe.Fori(1, NB) as i:
                rounds(i, True)
            project(NB)
            turn_tokens(NB)
            route(NB)
            reader = (diff_ready, NB)
            for c in range(NCH):
                for part in range(3):
                    reader = gate_up(NB, c, part, reader)
            hidden_out(NB, NCH - 2)
            hidden_out(NB, NCH - 1)
            turn_out(NB)

        @block.vector
        def _(dve):
            v = nc.vector
            v.memset(sig_bias[:], -SHARP * THRESH).then_inc(setup, 1)
            v.memset(AV[:], 0.0).then_inc(setup, 1)
            s_var, s_t, s_fac = (small[:, n, :] for n in range(3))

            def stats(link, src, first=0, count=SUB):
                for j in range(count):
                    ins = v.bn_stats(bst[:, j, :], src(j))
                    if j < count - 1:
                        link.count(ins)
                    else:
                        link(ins, alone=True)
                for j in range(count):
                    ins = v.bn_aggr(mv[:, first + j, :], bst[:, j, :])
                    if j < count - 1:
                        link.count(ins)
                    else:
                        link(ins)

            def variance(link, out, j0, j1, second):
                e = (1.0 + EPS, EPS * EPS) if second else (1.0, EPS)
                link(v.tensor_scalar(out, mv[:, j0:j1, 1], *e, ALU.mult, ALU.add))

            link = Steps(dve, pro, 0)

            def norms(j0, j1):
                stats(link, lambda j: x_sb[:, j0 + j, :], j0, j1 - j0)
                for n in (0, 1):
                    variance(link, var12[:, n, j0:j1], j0, j1, n)
                rsqrt(link, var12[:, :, j0:j1], fac12[:, :, j0:j1], fac_t[:, :, j0:j1])
                link(v.tensor_tensor(fac2[:, j0:j1], fac12[:, 0, j0:j1], var12[:, 0, j0:j1], ALU.mult))
                link(v.tensor_tensor(fac2[:, j0:j1], fac2[:, j0:j1], fac12[:, 1, j0:j1], ALU.mult))

            def tokens(b):
                wait(dve, hT_mm, b)
                for j in range(b * SUB, (b + 1) * SUB):
                    v.tensor_scalar(tok[:, j % SUB, :], x_sb[:, j, :], mv[:, j, 0:1], fac12[:, 0, j:j + 1],
                                    ALU.subtract, ALU.mult).then_inc(h_ready, 1)

            def set_up():
                dve.wait_ge(in_w, 6 * 16)
                v.tensor_copy(lnb_all[:], col(V_LNB).to_broadcast([P, P])).then_inc(setup, 1)
                dve.wait_ge(bias_mm, 1)
                v.tensor_copy(b_qk[:], GB[:, 0:2 * D]).then_inc(setup, 1)
                v.tensor_scalar(w_qkv[:, 0:2 * D], w_qkv[:, 0:2 * D], col(V_LNW), None, ALU.mult).then_inc(setup, 1)

            def gate_weights():
                v.tensor_copy(gq16[:, 0:1], col(V_GQ)).then_inc(setup, 1)
                dve.wait_ge(setup, 6)
                link(v.tensor_tensor(gq_parts[:, 0:1], col(V_GQ), gq16[:, 0:1], ALU.subtract))
                link(v.tensor_copy(gq16[:, 1:2], gq_parts[:, 0:1]))
                link(v.tensor_tensor(gq_parts[:, 1:2], gq_parts[:, 0:1], gq16[:, 1:2], ALU.subtract))
                link(v.tensor_copy(gq16[:, 2:3], gq_parts[:, 1:2]))
                link(v.tensor_copy(gq_parts[:, 2:5], gq16[:, 0:3]))
                link(v.tensor_scalar(gm_t[:], const_sb[:, C_MA:C_MA + P], gq_parts[:, 2:3], None, ALU.mult))
                v.scalar_tensor_tensor(out=gm_a[:], in0=const_sb[:, C_MB:C_MB + P], scalar=gq_parts[:, 3:4], in1=gm_t[:],
                                       op0=ALU.mult, op1=ALU.add).then_inc(setup, 1)
                v.tensor_scalar(gm_b[:], const_sb[:, C_MA:C_MA + P], gq_parts[:, 4:5], None, ALU.mult).then_inc(setup, 1)

            unit_k = qk[:, 1, :].rearrange("p (n d) -> p n d", d=HD)
            unit_q = qk[:, 0, :].rearrange("p (n d) -> p n d", d=HD)

            def unit(b):
                wait(dve, hi_ready, b * 4)
                for j in range(SUB):
                    dve.wait_ge(raw_ready, b * SUB + j + 1)
                    v.scalar_tensor_tensor(
                        out=qk[:, :, j * D:(j + 1) * D], in0=raw[b % 2][:, j, 0:2 * D].rearrange("p (w n) -> p w n", w=2),
                        scalar=fac2[:, b * SUB + j:b * SUB + j + 1], in1=b_qk[:].rearrange("p (w n) -> p w n", w=2),
                        op0=ALU.mult, op1=ALU.add).then_inc(qk_ready, 1)
                dve.wait_ge(qk_ready, b * SUB + SUB)
                dve.wait_ge(sq_ready, b + 1)
                ss = ssq[:].rearrange("p w n -> p (w n)")
                link(v.tensor_reduce(ss, sq, AX_X, ALU.add))
                link(v.tensor_scalar(ss, ss, NORM_EPS * NORM_EPS, None, ALU.max))
                rsqrt(link, ss, rn[:], rn_t[:])
                link(v.tensor_scalar(rn[:], rn[:], QK_SCALE, None, ALU.mult))
                both = qk.rearrange("p w n -> p (w n)").rearrange("p (n d) -> p n d", d=HD)
                v.tensor_tensor(both, both, rn[:].unsqueeze(2).to_broadcast([P, 2 * SUB * H, HD]), ALU.mult).then_inc(unit_ready, 1)
                dve.wait_ge(unit_ready, b + 1)

            def gated_values(b):
                gk = vec_sb[:, V_GK:V_GK + HD].unsqueeze(1).to_broadcast([P, SUB * H, HD])
                link(v.tensor_tensor(sq[:, 0:SUB * H, :], unit_k, gk, ALU.mult))
                link(v.tensor_reduce(gk_s[:], sq[:, 0:SUB * H, :], AX_X, ALU.add))
                link(v.tensor_scalar(gk_s[:], gk_s[:], 1.0 / QK_SCALE, None, ALU.mult))
                v.tensor_tensor(vg[:, b * SUB:(b + 1) * SUB, :, :],
                                raw[b % 2][:, :, 2 * D:3 * D].rearrange("p s (h d) -> p s h d", d=HD),
                                gk_s[:].rearrange("p (s h) -> p s h", s=SUB).unsqueeze(3).to_broadcast([P, SUB, H, HD]),
                                ALU.mult).then_inc(vg_ready, 1)

            def low_parts(b):
                dve.wait_ge(hi_ready, b * 4 + 4)
                for w, of, los in ((0, unit_q, (1, 3)), (1, unit_k, (2, 3))):
                    link(v.tensor_tensor(split[:, w, :, los[0], :], of, split[:, w, :, 0, :], ALU.subtract))
                    v.tensor_copy(split[:, w, :, los[1], :], split[:, w, :, los[0], :]).then_inc(lo_ready, 1)

            dve.wait_ge(in_x, 16)
            norms(0, SUB)
            tokens(0)
            set_up()
            dve.wait_ge(in_xs, 16)
            norms(SUB, ST)
            tokens(1)
            for b in range(NB):
                unit(b)
                if b + 2 < NB:
                    tokens(b + 2)
                gated_values(b)
                low_parts(b)
            gate_weights()

            def collapse(i, g):
                dve.wait_ge(av_mm, i * ROUNDS + (g + 1) * ST)
                dve.wait_ge(gateb_copied, i * NG + g + 1)
                if g == 0:
                    wait(dve, proj_mm, i)
                v.tensor_tensor(coll[:, g, :], AV[:], gate_q[:], ALU.mult).then_inc(coll_ready, 1)

            def attention_out(i, link):
                dve.wait_ge(proj_mm, i)
                bo = vec_sb[:, V_BO:V_BO + D].unsqueeze(1).to_broadcast([P, SUB, D])
                link(v.tensor_tensor(tok[:], GB[:].rearrange("p (s d) -> p s d", s=SUB), bo, ALU.add))
                stats(link, lambda j: tok[:, j, :])
                variance(link, s_var, 0, SUB, False)
                rsqrt(link, s_var, s_fac, s_t)
                for j in range(SUB):
                    ins = v.tensor_scalar(tok[:, j, :], tok[:, j, :], mv[:, j, 0:1], s_fac[:, j:j + 1], ALU.subtract, ALU.mult)
                    if j < SUB - 1:
                        link.count(ins)
                    else:
                        link(ins)
                link(v.tensor_tensor(x1, tok[:], x_sb[:, bass.ds((i - 1) * SUB, SUB), :], ALU.add))
                stats(link, lambda j: x1[:, j, :])
                variance(link, s_var, 0, SUB, True)
                rsqrt(link, s_var, s_fac, s_t)
                for j in range(SUB):
                    ins = v.tensor_scalar(tok[:, j, :], x1[:, j, :], mv[:, j, 0:1], s_fac[:, j:j + 1], ALU.subtract, ALU.mult)
                    if j < SUB - 1:
                        link.count(ins)
                    else:
                        ins.then_inc(n2_ready, 1)

            def expert_in(i):
                dve.wait_ge(n2_mm, i)
                v.tensor_scalar(xnT, UB[:], col(V_GAM), col(V_BET), ALU.mult, ALU.add).then_inc(xn_ready, 1)
                dve.wait_ge(xn_ready, i * 3 - 2)
                v.tensor_copy(xn_hi[:], xnT).then_inc(xn_ready, 1)
                dve.wait_ge(xn_ready, i * 3 - 1)
                v.tensor_tensor(xn_lo[:], xnT, xn_hi[:].bitcast(F32), ALU.subtract).then_inc(xn_ready, 1)

            def choose(i, link):
                dve.wait_ge(router_mm, i)
                link(v.tensor_copy(logit[:], GB[:, 0:SUB * E].rearrange("p (s e) -> p s e", s=SUB)), alone=True)
                for j in range(SUB):
                    ins = v.max(top[:, j, :], logit[:, j, :])
                    if j < SUB - 1:
                        link.count(ins)
                    else:
                        link(ins)
                v.tensor_tensor(tdiff[:], top[:, :, 1], top[:, :, 0], ALU.subtract).then_inc(diff_ready, 1)
                for j in range(SUB):
                    ins = v.max_index(topi[:, j, :], top[:, j, :], logit[:, j, :])
                    if j < SUB - 1:
                        link.count(ins)
                    else:
                        link(ins)
                link(v.tensor_copy(topf[:], topi[:, :, 0:2]))
                for n in (0, 1):
                    link(v.tensor_tensor(hot[:, n], iota.unsqueeze(1).to_broadcast([P, SUB, E]),
                                         topf[:, :, n:n + 1].to_broadcast([P, SUB, E]), ALU.is_equal))

            def combine(i, link):
                dve.wait_ge(twt_ready, i * 2)
                for n in (0, 1):
                    link(v.tensor_tensor(hot[:, n], hot[:, n], twt[:, n, :].unsqueeze(2).to_broadcast([P, SUB, E]), ALU.mult))
                v.tensor_tensor(hot[:, 2], hot[:, 0], hot[:, 1], ALU.add).then_inc(comb_ready, 1)

            def keep_comb(i):
                dve.wait_ge(combT_mm, i)
                v.tensor_copy(combT, GB[0:E, :]).then_inc(combT_ready, 1)

            def hidden(i, c, part):
                n = (i - 1) * NCH + c
                if part == 0:
                    dve.wait_ge(gate_mm, n + 1)
                    if c >= 2:
                        dve.wait_ge(sg_ready, n - 1)
                    v.tensor_scalar(gate_c[c % 2], GB[:], 10.0, -10.0, ALU.min, ALU.max).then_inc(gate_clipped, 1)
                else:
                    dve.wait_ge(up_mm, n + 1)
                    dve.wait_ge(gate_clipped, n + 1)
                    if c >= 2:
                        dve.wait_ge(hid_ready, n - 1)
                    v.tensor_tensor(prod[c % 2], gate_c[c % 2], UB[:], ALU.mult).then_inc(prod_ready, 1)

            def chunk_part(i, c, part, link):
                if part == 0:
                    hidden(i, c, 0)
                elif part == 1:
                    if c >= FC + 1 and (c - 1) % FC == 0:
                        add_expert(i, (c - 1) // FC - 1, link)
                else:
                    hidden(i, c, 2)
                    if c == COMB_CHUNK:
                        keep_comb(i)

            def add_expert(i, e, link):
                n = (i - 1) * (E + 1)
                dve.wait_ge(down_mm, (i - 1) * NCH + min((e + 1) * FC, NCH))
                if e < E:
                    dve.wait_ge(comb_in[e % 2], ((i - 1) * (E // 2) + e // 2 + 1) * 16)
                if e == 0:
                    v.tensor_tensor(acc, OB[:], comb_all[:, 0, :], ALU.mult).then_inc(acc_ready, 1)
                elif e < E:
                    link(v.tensor_tensor(tmp, OB[:], comb_all[:, e % 2, :], ALU.mult))
                    dve.wait_ge(acc_ready, n + e)
                    v.tensor_tensor(acc, acc, tmp, ALU.add).then_inc(acc_ready, 1)
                else:
                    dve.wait_ge(acc_ready, n + e)
                    v.tensor_tensor(acc, acc, OB[:], ALU.add).then_inc(acc_ready, 1)

            def finish(i, link):
                dve.wait_ge(fin_mm, i)
                stats(link, lambda j: UB[:, j * P:(j + 1) * P])
                variance(link, s_var, 0, SUB, False)
                rsqrt(link, s_var, s_fac, s_t)
                for j in range(SUB):
                    v.tensor_scalar(tok[:, j, :], UB[:, j * P:(j + 1) * P], mv[:, j, 0:1], s_fac[:, j:j + 1],
                                    ALU.subtract, ALU.mult).then_inc(fin_read, 1)
                dve.wait_ge(fin_read, i * SUB)
                v.tensor_tensor(tok[:], tok[:], x1, ALU.add).then_inc(out_ready, 1)

            def gates(i, g):
                dve.wait_ge(gateb_mm, i * NG + g + 1)
                wait(dve, coll_ready, i * NG + g)
                v.tensor_scalar(gate_q[:], GB[:], 1.0 / QK_SCALE, None, ALU.mult).then_inc(gateb_copied, 1)

            def rounds(i, experts):
                link = Steps(dve, blk, (i - 1) * BLK_STEPS) if experts else None
                for k in range(ROUNDS):
                    if experts:
                        if k == 0:
                            attention_out(i, link)
                        if k == TURN_ROUND:
                            expert_in(i)
                        if k == ROUTE_ROUND:
                            choose(i, link)
                            combine(i, link)
                        for c in range(NCH):
                            for part in range(3):
                                if unit_round(c, part) == k:
                                    chunk_part(i, c, part, link)
                        if k == unit_round(NCH, 0):
                            add_expert(i, E - 1, link)
                        if k == LAST_UNIT + 1:
                            add_expert(i, E, link)
                    if k % ST == 0 and k > 0:
                        collapse(i, k // ST - 1)
                    if k % ST == ST - 1:
                        gates(i, k // ST)
                collapse(i, NG - 1)
                if experts:
                    finish(i, link)
                    dve.wait_ge(out_saved, i * 16)
                    assert link.n == BLK_STEPS, link.n

            rounds(0, False)
            with dve.Fori(1, NB) as i:
                rounds(i, True)
            link = Steps(dve, blk, (NB - 1) * BLK_STEPS)
            attention_out(NB, link)
            expert_in(NB)
            choose(NB, link)
            combine(NB, link)
            for c in range(NCH):
                for part in range(3):
                    chunk_part(NB, c, part, link)
            add_expert(NB, E - 1, link)
            add_expert(NB, E, link)
            finish(NB, link)


def _layout(inputs):
    import numpy as np

    a = {k[3:]: np.asarray(v) for k, v in inputs.items()}
    f = np.float32
    rows = np.arange(P)
    same_head = rows[:, None] // 32 == rows[None, :] // 32
    first = (rows[:, None] % 32) < 16
    consts = np.concatenate([np.eye(P), same_head & first, same_head & ~first,
                             np.broadcast_to(np.arange(E), (P, E))], axis=1).astype(f)
    gq = np.tile(a["attn_gq"], P // HD)[:, None]
    gk = np.broadcast_to(a["attn_gk"], (P, HD))
    bo = np.broadcast_to(a["attn_bo"], (P, D))
    vecs = np.concatenate([a["attn_ln_w"][:, None], a["attn_ln_b"][:, None], a["ffn_ln_gamma"][:, None],
                           a["ffn_ln_beta"][:, None], gq, gk, bo], axis=1)
    wo = np.zeros((G, 32, NG, D), f)
    wo[:, :HD] = a["attn_Wo"].reshape(NG, G, HD, D).transpose(1, 2, 0, 3)
    gu = np.concatenate([a["ffn_gate_up_w"].transpose(1, 0, 2).reshape(D, E * 2 * F), a["ffn_shared_gate_up_w"]], axis=1)
    down = np.concatenate([a["ffn_down_w"].reshape(E * FC, P, D), a["ffn_shared_down_w"][None]]).transpose(1, 0, 2)
    return {
        "x": a["attn_x"].reshape(ST, P, D).transpose(1, 0, 2),
        "wqkv": np.concatenate([a["attn_Wq"], a["attn_Wk"], a["attn_Wv"]], axis=1),
        "vecs": vecs, "consts": consts, "ident16": np.eye(P, dtype=np.float16),
        "wo": wo.reshape(P, NG, D), "router": a["ffn_router_w"], "gu": gu, "down": down,
    }


def kernel(**inputs):
    import numpy as _np
    import concourse.bacc as _bacc
    from concourse import mybir as _mybir
    from concourse.bass_utils import run_bass_kernel_spmd as _run

    nc = _bacc.Bacc("TRN2", target_bir_lowering=False, num_devices=1)
    arrays, args = {}, []
    for name, a in _layout(inputs).items():
        a = _np.ascontiguousarray(a)
        arrays[f"in_{name}"] = a
        args.append(nc.dram_tensor(f"in_{name}", a.shape, _mybir.dt.from_np(a.dtype), kind="ExternalInput").ap())
    args.append(nc.dram_tensor("out_0", (P, ST, D), _mybir.dt.float32, kind="ExternalOutput").ap())
    build(nc, *args)
    r = _run(nc, [arrays], core_ids=[0])
    got = r.results[0]["out_0"]
    return got.transpose(1, 0, 2).reshape(1, T, D)
```

```python
from contextlib import ExitStack

import concourse.bass as bass
from concourse import mybir

P = 128
T = 2048
D = 128
H = 16
HD = D // H
SLOTS = 4
G = 4
NG = H // G
TB = 512
SUB = TB // P
NB = T // TB
ST = T // P
E = 8
F = 512
FC = F // P
NCH = E * FC + 1
GU = E * 2 * F + 2 * P
ROUNDS = NG * ST
LAG = 3
RING = LAG + 1
DEEP = 16

THRESH, SHARP, EPS, NORM_EPS = 0.29514, 15.0, 1e-5, 1e-12
QK_SCALE = 64.0
RSQRT_MAGIC = 1597463007.0

F32 = mybir.dt.float32
F32R = mybir.dt.float32r
F16 = mybir.dt.float16
BF16 = mybir.dt.bfloat16
I32 = mybir.dt.int32
U32 = mybir.dt.uint32
ALU = mybir.AluOpType
ACT = mybir.ActivationFunctionType
AX_X = mybir.AxisListType.X

LOW_SLOT, HIGH_AGAIN, LOW_AGAIN = (1, 2), (2, 1), (3, 3)

C_ID, C_MA, C_MB, C_IO = 0, P, 2 * P, 3 * P
V_LNW, V_LNB, V_GAM, V_BET, V_GQ, V_GK, V_BO = 0, 1, 2, 3, 4, 5, 5 + HD
NCONST, NVEC = 3 * P + E, 5 + HD + D

BLK_STEPS = 87

TURN_ROUND, ROUTE_ROUND, FIRST_UNIT, LAST_UNIT, FINISH_ROUND = 6, 8, 9, 57, 61
PROJECT_ROUND = 62
PROLOGUE = [("tokens", 0), ("project", 0), ("tokens", 1), ("square", 0), ("project", 1), ("high", 0),
            ("square", 1), ("turn", 0), ("tokens", 2), ("rounds", 1), ("high", 1), ("project", 2),
            ("square", 2), ("turn", 1), ("tokens", 3), ("rounds", 1), ("high", 2), ("project", 3), ("rounds", 1),
            ("square", 3), ("turn", 2), ("rounds", 2), ("high", 3), ("rounds", 3), ("turn", 3)]
WIDE_FROM, WIDE_TO = 9, 60
COMB_CHUNK = 1


def score_pair(n):
    return (n - 2 * WIDE_FROM) % 3 if 2 * WIDE_FROM <= n < 2 * WIDE_TO else n % 2


def scores_before(n):
    return max([m + 1 for m in range(n) if score_pair(m) == score_pair(n)], default=0)


def unit_round(c, part):
    return FIRST_UNIT + (3 * c + part) * (LAST_UNIT + 1 - FIRST_UNIT) // (3 * NCH)


def late_splits(start, c):
    return min(NCH, start + max(c + 1, 0) * (NCH - start) // (NCH - RING))


def added_after(c):
    return c // FC if c % FC == FC - 1 or c == NCH - 1 else None


def build(nc, x, wqkv, vecs, consts, ident16, wo, router, gu, down, out):
    ctx = ExitStack()
    with ctx:
        def sb(name, shape, dt=F32):
            return ctx.enter_context(nc.sbuf_tensor(name, shape, dt))

        def sem(name):
            return ctx.enter_context(nc.semaphore(name))

        x_sb = sb("x_sb", [P, ST, D])
        const_sb = sb("const_sb", [P, NCONST])
        vec_sb = sb("vec_sb", [P, NVEC])
        id16 = sb("id16", [P, P], F16)
        w_qkv = sb("w_qkv", [P, 3 * D])
        wo_sb = sb("wo_sb", [P, NG, D])
        rw_sb = sb("rw_sb", [P, E])
        lnb_all = sb("lnb_all", [P, P])
        b_qk = sb("b_qk", [P, 2 * D])
        gu_sb = sb("gu_sb", [P, GU])
        gu_hi = sb("gu_hi", [P, 2, 2, P], F32R)
        gu_lo = sb("gu_lo", [P, 2, 2, P], F32R)
        down_hi = sb("down_hi", [P, RING, D], F32R)
        down_lo = sb("down_lo", [P, RING, D], F32R)
        hid_hi = sb("hid_hi", [P, LAG, TB], F32R)
        hid_lo = sb("hid_lo", [P, LAG, TB], F32R)
        down_sb = sb("down_sb", [P, NCH, D])
        vg = sb("vg", [P, ST, H, HD])
        qT = sb("qT", [P, NG, TB], F16)
        coll = sb("coll", [P, NG, TB])
        gate_q = sb("gate_q", [P, TB])
        gq_parts = sb("gq_parts", [P, 8])
        gq16 = sb("gq16", [P, 3], BF16)
        gm_a = sb("gm_a", [P, P], BF16)
        gm_b = sb("gm_b", [P, P], BF16)
        gm_t = sb("gm_t", [P, P])
        sig_bias = sb("sig_bias", [P, 1])
        tok = sb("tok", [P, SUB, D])
        xn_hi = sb("xn_hi", [P, TB], F32R)
        xn_lo = sb("xn_lo", [P, TB], F32R)
        comb_all = sb("comb_all", [P, 2, TB])
        bst = sb("bst", [P, ST - SUB, 6])
        mv = sb("mv", [P, ST, 2])
        small = sb("small", [P, 3, SUB])
        var12 = sb("var12", [P, 2, ST])
        fac12 = sb("fac12", [P, 2, ST])
        fac_t = sb("fac_t", [P, 2, ST])
        fac2 = sb("fac2", [P, ST])
        logit = sb("logit", [P, SUB, E])
        top = sb("top", [P, SUB, 8])
        topi = sb("topi", [P, SUB, 8], U32)
        topf = sb("topf", [P, SUB, 2])
        pause = sb("pause", [P, 1])
        tdiff = sb("tdiff", [P, SUB])
        twt = sb("twt", [P, 2, SUB])
        hot = sb("hot", [P, 3, SUB, E])
        work = sb("work", [P, 12 * TB])
        gate_c = [work[:, n * TB:(n + 1) * TB] for n in (0, 1)]
        prod = [work[:, n * TB:(n + 1) * TB] for n in (2, 3)]
        sg = [work[:, n * TB:(n + 1) * TB] for n in (4, 5)]
        hid = [work[:, n * TB:(n + 1) * TB] for n in (6, 7)]
        x1 = work[:, 8 * TB:9 * TB].rearrange("p (s d) -> p s d", s=SUB)
        acc = work[:, 9 * TB:10 * TB]
        tmp = work[:, 10 * TB:11 * TB]
        xnT = work[:, 11 * TB:12 * TB]
        result = xnT.rearrange("p (s d) -> p s d", s=SUB)
        combT = tmp[0:E, :]
        hT = work[:, 0:TB]
        raw = [m.rearrange("p (s n) -> p s n", s=SUB)
               for m in (work[:, TB:4 * TB], coll[:, 0:3, :].rearrange("p g t -> p (g t)"))]
        q_out = comb_all[:].rearrange("p n t -> p (n t)").bitcast(F16).rearrange("p (g t) -> p g t", g=NG)
        qk = work[:, 4 * TB:6 * TB].rearrange("p (w n) -> p w n", w=2)
        sq = work[:, 6 * TB:8 * TB].rearrange("p (n d) -> p n d", d=HD)
        split = work[:, 8 * TB:12 * TB].bitcast(F16).rearrange(
            "p (w n s d) -> p w n s d", w=2, s=SLOTS, d=HD)
        NQK = 2 * SUB * H
        ssq = sb("ssq", [P, NQK])
        rn = sb("rn", [P, NQK])
        rn_t = sb("rn_t", [P, NQK])
        gk_prod = sb("gk_prod", [P, SUB * H, HD])
        gk_s = sb("gk_s", [P, SUB * H])

        q_dram = nc.dram_tensor("q_dram", (NB, P, NG, TB), F16).ap()
        comb_dram = nc.dram_tensor("comb_dram", (E, TB), F32).ap()

        with (nc.sbuf_tensor("kT", [P, NG, T], F16) as kT, nc.sbuf_tensor("q_pad", [P, NG, G, TB], F16) as q_pad,
              nc.sbuf_tensor("res", [P, 2, G, TB], F32) as res):
            pass
        late_gu = sb("late_gu", [P, DEEP, 2, 2, P], F32R)
        late_down = sb("late_down", [P, DEEP, 2, P], F32R)

        S = ctx.enter_context(nc.psum_tensor("S", [P, G, TB], F32))
        AV = ctx.enter_context(nc.psum_tensor("AV", [P, TB], F32))
        GB = ctx.enter_context(nc.psum_tensor("GB", [P, TB], F32))
        UO = ctx.enter_context(nc.psum_tensor("UO", [P, 2, TB], F32))
        UB, OB = UO[:, 0, :], UO[:, 1, :]

        ident = const_sb[:, C_ID:C_ID + P]
        iota = const_sb[:, C_IO:C_IO + E]

        def col(n):
            return vec_sb[:, n:n + 1]

        in_x = sem("in_x")
        in_xs = sem("in_xs")
        in_const = sem("in_const")
        in_qkv = sem("in_qkv")
        in_w = sem("in_w")
        in_down = sem("in_down")
        in_gu = sem("in_gu")
        zeroed = sem("zeroed")
        setup = sem("setup")
        bias_mm = sem("bias_mm")
        pro = sem("pro")
        h_ready = sem("h_ready")
        hT_mm = sem("hT_mm")
        hT_ready = sem("hT_ready")
        qkv_mm = sem("qkv_mm")
        raw_ready = sem("raw_ready")
        qk_ready = sem("qk_ready")
        sq_ready = sem("sq_ready")
        unit_ready = sem("unit_ready")
        hi_ready = sem("hi_ready")
        lo_ready = sem("lo_ready")
        repeated = sem("repeated")
        vg_ready = sem("vg_ready")
        qk_tr = sem("qk_tr")
        qk_copied = sem("qk_copied")
        q_saved = sem("q_saved")
        q0_staged = sem("q0_staged")
        act_warm = sem("act_warm")
        q_staged = [sem(f"q_staged{g}") for g in range(NG)]
        gu_high = sem("gu_high")
        gu_split = sem("gu_split")
        down_high = sem("down_high")
        down_split = sem("down_split")
        score_mm = sem("score_mm")
        sig_done = sem("sig_done")
        av_mm = sem("av_mm")
        gateb_mm = sem("gateb_mm")
        gateb_copied = sem("gateb_copied")
        coll_ready = sem("coll_ready")
        proj_mm = sem("proj_mm")
        blk = sem("blk")
        n2_ready = sem("n2_ready")
        n2_mm = sem("n2_mm")
        xn_ready = sem("xn_ready")
        router_mm = sem("router_mm")
        diff_ready = sem("diff_ready")
        twt_ready = sem("twt_ready")
        comb_ready = sem("comb_ready")
        combT_mm = sem("combT_mm")
        combT_ready = sem("combT_ready")
        comb_saved = sem("comb_saved")
        comb_in = [sem("comb_in0"), sem("comb_in1")]
        gate_mm = sem("gate_mm")
        up_mm = sem("up_mm")
        gate_clipped = sem("gate_clipped")
        prod_ready = sem("prod_ready")
        sg_ready = sem("sg_ready")
        hid_ready = sem("hid_ready")
        hid_high = sem("hid_high")
        hid_split = sem("hid_split")
        down_mm = sem("down_mm")
        acc_ready = sem("acc_ready")
        fin_mm = sem("fin_mm")
        fin_read = sem("fin_read")
        out_ready = sem("out_ready")
        out_saved = sem("out_saved")

        def late(i):
            return isinstance(i, int) and i == NB

        def split_gu(i, c):
            if late(i):
                return late_gu[:, c % DEEP, 0], late_gu[:, c % DEEP, 1]
            return gu_hi[:, c % 2], gu_lo[:, c % 2]

        def split_dn(i, c):
            if late(i):
                return late_down[:, c % DEEP, 0], late_down[:, c % DEEP, 1]
            return down_hi[:, c % RING], down_lo[:, c % RING]

        def gate_up_of(c):
            if c < E * FC:
                both = gu_sb[:, c // FC * 2 * F:(c // FC + 1) * 2 * F].rearrange("p (w n) -> p w n", w=2)
                return both[:, :, c % FC * P:(c % FC + 1) * P]
            return gu_sb[:, E * 2 * F:GU].rearrange("p (w n) -> p w n", w=2)

        def gate_bank(i, c):
            return S[:, 0, :] if late(i) and c % 2 else GB[:]

        def up_bank(i, c):
            return S[:, 1, :] if late(i) and c % 2 else UB

        def out_bank(i, e):
            return S[:, 2, :] if late(i) and e % 2 else OB

        def score_banks(i, k, half):
            pair = score_pair(2 * k + half) if isinstance(i, int) else half
            return UO[:] if pair == 2 else S[:, 2 * pair:2 * pair + 2, :]

        def turned_bank(b, n):
            dst = (q_out if b else qT[:]) if n < 2 else kT[:, :, b * TB:(b + 1) * TB]
            return dst[:, 2 * (n % 2):2 * (n % 2) + 2, :], (UB, OB)[n % 2].bitcast(F16).rearrange("p (g t) -> p g t", g=2)

        def rsqrt(link, v, y, t):
            link(nc.vector.tensor_scalar(t.bitcast(I32), v.bitcast(I32), 1, None, ALU.logical_shift_right))
            link(nc.vector.tensor_scalar(y.bitcast(I32), t.bitcast(I32), -1.0, RSQRT_MAGIC, ALU.mult, ALU.add))
            link(nc.vector.tensor_tensor(t, y, y, ALU.mult))
            link(nc.vector.tensor_tensor(t, t, v, ALU.mult))
            link(nc.vector.scalar_tensor_tensor(out=t, in0=t, scalar=-10.0 / 3, in1=t, op0=ALU.add, op1=ALU.mult))
            link(nc.vector.scalar_tensor_tensor(out=y, in0=t, scalar=5.0, in1=y, op0=ALU.add, op1=ALU.mult))
            link(nc.vector.scalar_tensor_tensor(out=t, in0=y, scalar=-0.5 * 0.375 ** 3, in1=y, op0=ALU.mult, op1=ALU.mult))
            link(nc.vector.tensor_tensor(t, t, v, ALU.mult))
            link(nc.vector.scalar_tensor_tensor(out=y, in0=t, scalar=1.5 * 0.375, in1=y, op0=ALU.add, op1=ALU.mult))

        class Steps:

            def __init__(self, eng, s, base):
                self.eng, self.s, self.base, self.n = eng, s, base, 0

            def count(self, ins):
                self.n += 1
                ins.then_inc(self.s, 1)

            def after(self, n):
                self.eng.wait_ge(self.s, self.base + n)

            def __call__(self, ins, alone=False):
                self.count(ins)
                self.eng.wait_ge(self.s, self.base + self.n)
                if alone:
                    self.eng.memset(pause[:], 0.0)

        def wait(eng, s, value):
            if not isinstance(value, int) or value > 0:
                eng.wait_ge(s, value)

        block = ctx.enter_context(nc.Block())

        @block.sync
        def _(sp):
            sp.dma_start(x_sb[:, 0:SUB, :], x[:, 0:SUB, :]).then_inc(in_x, 16)
            sp.dma_start(w_qkv[:], wqkv).then_inc(in_qkv, 16)
            for dst, src in ((wo_sb, wo), (rw_sb, router)):
                sp.dma_start(dst[:], src).then_inc(in_w, 16)
            sp.dma_start(x_sb[:, SUB:ST, :], x[:, SUB:ST, :]).then_inc(in_xs, 16)
            sp.dma_start(gu_sb[:], gu).then_inc(in_gu, 16)
            sp.dma_start(down_sb[:], down).then_inc(in_down, 16)
            sp.wait_ge(zeroed, 1)
            sp.wait_ge(qk_copied, 2)
            for j in range(G):
                r = slice(32 * j, 32 * j + 32)
                sp.dma_start(q_pad[r, :, j, :], qT[r, :, :]).then_inc(q0_staged, 16)
            for b in range(NB):
                sp.wait_ge(qk_copied, 4 * b + 2)
                sp.dma_start(q_dram[b], q_out if b else qT[:]).then_inc(q_saved, 16)
            def stage(i, g, nxt):
                sp.wait_ge(gateb_mm, i * NG + g + 1)
                if isinstance(nxt, int):
                    src = q_dram[nxt]
                else:
                    src = q_dram[bass.ds(nxt, 1)].rearrange("o p g t -> (o p) g t")
                for j in range(G):
                    r = slice(32 * j, 32 * j + 32)
                    sp.dma_start(q_pad[r, g, j, :], src[r, g, :]).then_inc(q_staged[g], 16)
                sp.dma_start(qT[:, g, :], src[:, g, :]).then_inc(q_staged[g], 16)

            def experts(i, attention):
                nxt = sp.snap((i + 1) % NB) if attention else None
                sp.wait_ge(combT_ready, i)
                sp.dma_start(comb_dram, combT).then_inc(comb_saved, 16)
                sp.wait_ge(comb_saved, i * 16)
                staged = 0
                for e in range(E):
                    while attention and e >= 2 and (staged + 1) * ST < unit_round(FC * (e - 1) - 1 + LAG, 1):
                        stage(i, staged, nxt)
                        staged += 1
                    if e >= 2:
                        sp.wait_ge(acc_ready, (i - 1) * (E + 1) + e - 1)
                    sp.dma_start(comb_all[:, e % 2, :], comb_dram[e, :].partition_broadcast(P)).then_inc(comb_in[e % 2], 16)
                for g in range(staged, NG if attention else 0):
                    stage(i, g, nxt)
                sp.wait_ge(out_ready, i)
                sp.dma_start(out[:, bass.ds((i - 1) * SUB, SUB), :], result).then_inc(out_saved, 16)

            sp.wait_ge(q_saved, 16 * NB)
            for g in range(NG):
                stage(0, g, 1)
            with sp.Fori(1, NB) as i:
                experts(i, True)
            experts(NB, False)
            sp.wait_ge(out_saved, 16 * (NB + 1))
            for g in range(NG):
                sp.wait_ge(q_staged[g], NB * 5 * 16)

        @block.gpsimd
        def _(pool):
            nc.gpsimd.memset(q_pad[:].rearrange("p g j t -> p (g j t)").bitcast(F32), 0.0).then_inc(zeroed, 1)
            for b in range(NB):
                for done, src, dst in ((hi_ready, (0, 0), HIGH_AGAIN), (lo_ready, LOW_SLOT, LOW_AGAIN)):
                    for w in (0, 1):
                        pool.wait_ge(done, b * 2 + w + 1)
                        nc.gpsimd.tensor_scalar(split[:, w, :, dst[w], :], split[:, w, :, src[w], :], 1.0, 0.0,
                                                ALU.mult, ALU.add).then_inc(repeated, 1)
            pool.wait_ge(in_gu, 16)
            pool.wait_ge(in_down, 16)

            def split_gate_up(i, c):
                hi, lo = split_gu(i, c)
                w = gate_up_of(c)
                if not late(i):
                    nc.gpsimd.tensor_scalar(hi, w, 1.0, 0.0, ALU.mult, ALU.add).then_inc(gu_high, 1)
                pool.wait_ge(gu_high, (i - 1) * NCH + c + 1)
                nc.gpsimd.tensor_tensor(lo, w, hi.bitcast(F32), ALU.subtract).then_inc(gu_split, 1)

            def split_down(i, c):
                hi, lo = split_dn(i, c)
                w = down_sb[:, c, :]
                if not late(i):
                    nc.gpsimd.tensor_scalar(hi, w, 1.0, 0.0, ALU.mult, ALU.add).then_inc(down_high, 1)
                pool.wait_ge(down_high, (i - 1) * NCH + c + 1)
                nc.gpsimd.tensor_tensor(lo, w, hi.bitcast(F32), ALU.subtract).then_inc(down_split, 1)

            def experts(i):
                gu_ahead, down_ahead = (DEEP, DEEP - RING) if late(i) else (2, 0)
                for c in range(gu_ahead):
                    split_gate_up(i, c)
                for c in range(down_ahead):
                    split_down(i, c)
                for c in range(NCH):
                    n = (i - 1) * NCH + c
                    pool.wait_ge(prod_ready, n + 1)
                    pool.wait_ge(sg_ready, n + 1)
                    if c >= 2:
                        pool.wait_ge(hid_split, n - 1)
                    if c >= RING:
                        pool.wait_ge(down_mm, n - RING + 1)
                    nc.gpsimd.tensor_tensor(hid[c % 2], prod[c % 2], sg[c % 2], ALU.mult).then_inc(hid_ready, 1)
                    if late(i):
                        for n in range(late_splits(gu_ahead, c - 2), late_splits(gu_ahead, c - 1)):
                            split_gate_up(i, n)
                        for n in range(late_splits(down_ahead, c - 2), late_splits(down_ahead, c - 1)):
                            split_down(i, n)
                    else:
                        if c + gu_ahead < NCH:
                            split_gate_up(i, c + gu_ahead)
                        split_down(i, c)

            with pool.Fori(1, NB) as i:
                experts(i)
            pool.wait_ge(av_mm, NB * ROUNDS)
            for g in range(NG):
                pool.wait_ge(q_staged[g], NB * 5 * 16)
            experts(NB)

        @block.scalar
        def _(act):
            for dst, src in ((const_sb, consts), (vec_sb, vecs), (id16, ident16)):
                act.dma_start(dst[:], src).then_inc(in_const, 16)
            act.wait_ge(setup, 1)
            nc.scalar.activation(twt[:, 0, 0:1], sig_bias[:], ACT.Sigmoid).then_inc(act_warm, 1)

            def transposed(b):
                act.wait_ge(hT_mm, b + 1)
                wait(act, qkv_mm, b * SUB)
                nc.scalar.activation(hT, UB, ACT.Copy).then_inc(hT_ready, 1)

            def project(b):
                if b >= 2:
                    act.wait_ge(vg_ready, b - 1)
                for j in range(SUB):
                    act.wait_ge(qkv_mm, b * SUB + j + 1)
                    nc.scalar.activation(raw[b % 2][:, j, :], (GB, OB)[j % 2][:, 0:3 * D], ACT.Copy).then_inc(raw_ready, 1)

            def square(b):
                act.wait_ge(qk_ready, b * SUB + SUB)
                nc.scalar.activation(sq, qk.rearrange("p w n -> p (w n)").rearrange("p (n d) -> p n d", d=HD),
                                     ACT.Square).then_inc(sq_ready, 1)

            def high_parts(b):
                act.wait_ge(unit_ready, b + 1)
                for w in (0, 1):
                    nc.scalar.activation(split[:, w, :, 0, :], qk[:, w, :].rearrange("p (n d) -> p n d", d=HD),
                                         ACT.Copy).then_inc(hi_ready, 1)

            def turn(b):
                for n in range(4):
                    if n == 0 and b >= 2:
                        act.wait_ge(q_saved, b * 16)
                    act.wait_ge(qk_tr, b * 4 + n + 1)
                    nc.scalar.activation(*turned_bank(b, n), ACT.Copy).then_inc(qk_copied, 1)

            def silu(i, c):
                n = (i - 1) * NCH + c
                act.wait_ge(gate_clipped, n + 1)
                if c >= 2:
                    act.wait_ge(hid_ready, n - 1)
                nc.scalar.activation(sg[c % 2], gate_c[c % 2], ACT.Sigmoid).then_inc(sg_ready, 1)

            def hidden_high(i, c):
                n = (i - 1) * NCH + c
                act.wait_ge(hid_ready, n + 1)
                if c >= LAG:
                    act.wait_ge(down_mm, n - LAG + 1)
                nc.scalar.activation(hid_hi[:, c % LAG], hid[c % 2], ACT.Copy).then_inc(hid_high, 1)

            def high_gate_up(i, c):
                nc.scalar.activation(split_gu(i, c)[0], gate_up_of(c), ACT.Copy).then_inc(gu_high, 1)

            def high_down(i, c):
                nc.scalar.activation(split_dn(i, c)[0], down_sb[:, c, :], ACT.Copy).then_inc(down_high, 1)

            def top_weights(i):
                act.wait_ge(diff_ready, i)
                nc.scalar.activation(twt[:, 0, :], tdiff[:], ACT.Sigmoid, scale=-1.0).then_inc(twt_ready, 1)
                nc.scalar.activation(twt[:, 1, :], tdiff[:], ACT.Sigmoid).then_inc(twt_ready, 1)

            def sigmoids(i, k):
                for half in (0, 1):
                    act.wait_ge(score_mm, i * 2 * ROUNDS + 2 * k + half + 1)
                    if half == 0:
                        wait(act, av_mm, i * ROUNDS + k - 1)
                    nc.scalar.activation(
                        res[:, k % 2, 2 * half:2 * half + 2, :].rearrange("p h t -> p (h t)"),
                        score_banks(i, k, half).rearrange("p h t -> p (h t)"), ACT.Sigmoid,
                        bias=-SHARP * THRESH, scale=SHARP / (QK_SCALE * QK_SCALE)).then_inc(sig_done, 1)

            def rounds(i, experts, first=0):
                for k in range(first, ROUNDS):
                    sigmoids(i, k)
                    if experts:
                        if k == ROUTE_ROUND:
                            top_weights(i)
                        for c in range(NCH):
                            if unit_round(c, 2) + 1 == k:
                                hidden_high(i, c)
                            if unit_round(c, 0) == k:
                                silu(i, c)

            done = 0
            for what, b in PROLOGUE:
                if what == "rounds":
                    for k in range(done, done + b):
                        sigmoids(0, k)
                    done += b
                else:
                    if (what, b) == ("turn", NB - 1):
                        continue
                    {"tokens": transposed, "project": project, "square": square, "high": high_parts, "turn": turn}[what](b)
            rounds(0, False, done)
            with act.Fori(1, NB) as i:
                rounds(i, True)
            act.wait_ge(av_mm, NB * ROUNDS)
            for g in range(NG):
                act.wait_ge(q_staged[g], NB * 5 * 16)
            for c in range(DEEP):
                high_gate_up(NB, c)
            for c in range(DEEP - RING):
                high_down(NB, c)
            top_weights(NB)
            for c in range(NCH + 1):
                if c < NCH:
                    silu(NB, c)
                if c > 0:
                    hidden_high(NB, c - 1)
                    for n in range(late_splits(DEEP, c - 2), late_splits(DEEP, c - 1)):
                        high_gate_up(NB, n)
                    for n in range(late_splits(DEEP - RING, c - 2), late_splits(DEEP - RING, c - 1)):
                        high_down(NB, n)

        @block.tensor
        def _(pe):
            pe.wait_ge(setup, 3)
            pe.wait_ge(in_qkv, 16)
            pe.wait_ge(in_const, 3 * 16)
            nc.tensor.matmul(GB[:, 0:2 * D], lnb_all[:], w_qkv[:, 0:2 * D], start=True, stop=True).then_inc(bias_mm, 1)

            def turn_hidden(b, turned):
                pe.wait_ge(h_ready, b * SUB + SUB)
                wait(pe, qk_copied, 4 * turned)
                wait(pe, hT_ready, b)
                for j in range(SUB):
                    mm = nc.tensor.transpose(UB[:, j * P:(j + 1) * P], tok[:, j, :], ident)
                mm.then_inc(hT_mm, 1)

            def project_qkv(b, turned):
                pe.wait_ge(hT_ready, b + 1)
                if b == 0:
                    pe.wait_ge(setup, 5)
                wait(pe, qk_copied, 4 * turned)
                for j in range(SUB):
                    wait(pe, raw_ready, max(b * SUB + j - 1, 0))
                    nc.tensor.matmul((GB, OB)[j % 2][:, 0:3 * D], hT[:, j * P:(j + 1) * P], w_qkv[:],
                                     start=True, stop=True).then_inc(qkv_mm, 1)

            def turn_qk(b, projected, tokens):
                pe.wait_ge(raw_ready, projected * SUB)
                pe.wait_ge(hT_ready, tokens)
                pe.wait_ge(hi_ready, b * 2 + 2)
                for n in range(4):
                    pe.wait_ge(lo_ready, b * 2 + n // 2 + 1)
                    pe.wait_ge(repeated, b * 4 + n // 2 + 3)
                    if n >= 2:
                        pe.wait_ge(qk_copied, b * 4 + n - 1)
                    bank = (UB, OB)[n % 2][:].bitcast(F16)
                    for gg in (0, 1):
                        for j in range(SUB):
                            first = j * H + (2 * (n % 2) + gg) * G
                            mm = nc.tensor.transpose(
                                bank[:, gg * TB + j * P:gg * TB + (j + 1) * P],
                                split[:, n // 2, first:first + G, :, :].rearrange("p n s d -> p (n s d)"), id16[:])
                    mm.then_inc(qk_tr, 1)

            def scores(i, k):
                g, s = k // ST, k % ST
                if isinstance(i, int) and i == 0:
                    pe.wait_ge(qk_copied, 4 * (s // SUB + 1))
                    pe.wait_ge(q0_staged, 16 * G)
                elif s == 0:
                    pe.wait_ge(q_staged[g], i * 5 * 16)
                for j in range(G):
                    if j % 2 == 0:
                        if isinstance(i, int):
                            wait(pe, sig_done, scores_before(2 * k + j // 2))
                        else:
                            pe.wait_ge(sig_done, i * 2 * ROUNDS + 2 * k + j // 2 - 1)
                        if isinstance(i, int) and (k, j) == (WIDE_FROM, 0):
                            pe.wait_ge(qk_copied, 4 * NB)
                        banks = score_banks(i, k, j // 2)
                    mm = nc.tensor.matmul(banks[:, j % 2, :], kT[:, g, s * P:(s + 1) * P], q_pad[:, g, j, :], start=True, stop=True)
                    if j % 2 == 1:
                        mm.then_inc(score_mm, 1)

            def values(i, k):
                g, s = k // ST, k % ST
                if s == 0:
                    wait(pe, coll_ready, i * NG + g)
                if isinstance(i, int) and i == 0:
                    pe.wait_ge(vg_ready, s // SUB + 1)
                for j in range(G):
                    if j % 2 == 0:
                        pe.wait_ge(sig_done, i * 2 * ROUNDS + 2 * k + j // 2 + 1)
                    mm = nc.tensor.matmul(AV[32 * j:32 * j + HD, :], vg[:, s, G * g + j, :], res[:, k % 2, j, :],
                                          start=s == 0, stop=s == ST - 1)
                mm.then_inc(av_mm, 1)

            def gate_rows(i, g, before):
                pe.wait_ge(*before)
                if isinstance(i, int) and g == 0:
                    pe.wait_ge(setup, 8)
                nc.tensor.matmul(GB[:], gm_a[:], qT[:, g, :], start=True, stop=False)
                nc.tensor.matmul(GB[:], gm_b[:], qT[:, g, :], start=False, stop=True).then_inc(gateb_mm, 1)

            def project_first(i, bank_reader):
                pe.wait_ge(coll_ready, i * NG + NG - 1)
                pe.wait_ge(*bank_reader)
                if isinstance(i, int):
                    pe.wait_ge(in_w, 2 * 16)
                    pe.wait_ge(sig_done, 2 * WIDE_TO)
                for j in range(SUB):
                    for g in range(NG - 1):
                        nc.tensor.matmul(OB[:, j * D:(j + 1) * D], coll[:, g, j * P:(j + 1) * P], wo_sb[:, g, :],
                                         start=g == 0 and j == 0, stop=False)

            def project_last(i):
                pe.wait_ge(coll_ready, i * NG)
                for j in range(SUB):
                    mm = nc.tensor.matmul(OB[:, j * D:(j + 1) * D], coll[:, NG - 1, j * P:(j + 1) * P], wo_sb[:, NG - 1, :],
                                          start=False, stop=j == SUB - 1)
                mm.then_inc(proj_mm, 1)

            def turn_tokens(i):
                pe.wait_ge(n2_ready, i)
                for j in range(SUB):
                    mm = nc.tensor.transpose(UB[:, j * P:(j + 1) * P], tok[:, j, :], ident)
                mm.then_inc(n2_mm, 1)

            def route(i):
                pe.wait_ge(xn_ready, i * 3)
                for j in range(SUB):
                    mm = nc.tensor.matmul(OB[:, j * E:(j + 1) * E], xnT[:, j * P:(j + 1) * P], rw_sb[:], start=True, stop=True)
                mm.then_inc(router_mm, 1)

            def turn_comb(i):
                pe.wait_ge(comb_ready, i)
                for j in range(SUB):
                    mm = nc.tensor.matmul(OB[0:E, j * P:(j + 1) * P], hot[:, 2, j, :], ident, start=True, stop=True)
                mm.then_inc(combT_mm, 1)

            def three_passes(bank, w_hi, w_lo, v_hi, v_lo, first=True, last=True):
                for n, (w, v) in enumerate(((w_hi, v_hi), (w_hi, v_lo), (w_lo, v_hi))):
                    mm = nc.tensor.matmul(bank, w, v, start=first and n == 0, stop=last and n == 2)
                return mm

            def gate_up(i, c, part, gate_reader):
                n = (i - 1) * NCH + c
                hi, lo = split_gu(i, c)
                if part == 0:
                    if late(i) and c > 0:
                        gate_reader = (gate_clipped, n - 1)
                    pe.wait_ge(*gate_reader)
                    pe.wait_ge(gu_split, n + 1)
                    three_passes(gate_bank(i, c), hi[:, 0], lo[:, 0], xn_hi[:], xn_lo[:]).then_inc(gate_mm, 1)
                    return gate_clipped, n + 1
                if part == 1:
                    if c >= LAG:
                        hidden_out(i, c - LAG)
                    return gate_reader
                if c == 0:
                    pe.wait_ge(xn_ready, i * 3)
                else:
                    pe.wait_ge(prod_ready, n - 1 if late(i) else n)
                three_passes(up_bank(i, c), hi[:, 1], lo[:, 1], xn_hi[:], xn_lo[:]).then_inc(up_mm, 1)
                if c == COMB_CHUNK:
                    turn_comb(i)
                return gate_reader

            def hidden_out(i, c):
                e = c // FC
                pe.wait_ge(hid_split, (i - 1) * NCH + c + 1)
                pe.wait_ge(down_split, (i - 1) * NCH + c + 1)
                if c % FC == 0 and c > 0:
                    pe.wait_ge(acc_ready, (i - 1) * (E + 1) + (e - 1 if late(i) else e))
                hi, lo = split_dn(i, c)
                three_passes(out_bank(i, e), hi, lo, hid_hi[:, c % LAG], hid_lo[:, c % LAG],
                             c % FC == 0, added_after(c) is not None).then_inc(down_mm, 1)

            def turn_out(i):
                pe.wait_ge(acc_ready, i * (E + 1))
                for j in range(SUB):
                    mm = nc.tensor.transpose(UB[:, j * P:(j + 1) * P], acc[:, j * P:(j + 1) * P], ident)
                mm.then_inc(fin_mm, 1)

            def rounds(i, experts, first=0):
                reader = (gateb_copied, i * NG) if experts else (qk_copied, 4 * NB)
                for k in range(first, ROUNDS):
                    scores(i, k)
                    if experts:
                        if k == 0:
                            project_last(i)
                        if k == TURN_ROUND:
                            turn_tokens(i)
                        if k == ROUTE_ROUND:
                            route(i)
                        for c in range(NCH):
                            for part in range(3):
                                if unit_round(c, part) == k:
                                    reader = gate_up(i, c, part, reader)
                        if LAST_UNIT < k <= LAST_UNIT + LAG:
                            hidden_out(i, NCH - LAG + k - LAST_UNIT - 1)
                        if k == FINISH_ROUND:
                            turn_out(i)
                    if k == PROJECT_ROUND:
                        project_first(i, (acc_ready, i * (E + 1)) if experts else (qk_copied, 4 * NB))
                    if k > 0:
                        values(i, k - 1)
                    if k % ST == ST - 1:
                        gate_rows(i, k // ST, reader)
                        reader = (gateb_copied, i * NG + k // ST + 1)
                values(i, ROUNDS - 1)

            done, tokens, projected, turned = 0, 0, 0, 0
            for what, b in PROLOGUE:
                if what == "tokens":
                    turn_hidden(b, turned)
                    tokens += 1
                elif what == "project":
                    project_qkv(b, turned)
                    projected += 1
                elif what == "turn":
                    turn_qk(b, projected, tokens)
                    turned += 1
                elif what == "rounds":
                    for k in range(done, done + b):
                        scores(0, k)
                        if k > 0:
                            values(0, k - 1)
                    done += b
            rounds(0, False, done)
            with pe.Fori(1, NB) as i:
                rounds(i, True)
            project_last(NB)
            turn_tokens(NB)
            route(NB)
            reader = (gateb_copied, NB * NG)
            for c in range(NCH):
                for part in range(3):
                    reader = gate_up(NB, c, part, reader)
            for c in range(NCH - LAG, NCH):
                hidden_out(NB, c)
            turn_out(NB)

        @block.vector
        def _(dve):
            v = nc.vector
            v.memset(sig_bias[:], -SHARP * THRESH).then_inc(setup, 1)
            v.memset(AV[:], 0.0).then_inc(setup, 1)
            v.memset(pause[:], 0.0).then_inc(out_saved, 16)
            s_var, s_t, s_fac = (small[:, n, :] for n in range(3))

            def stats(link, src, first=0, count=SUB):
                for j in range(count):
                    ins = v.bn_stats(bst[:, j, :], src(j))
                    if j < count - 1:
                        link.count(ins)
                    else:
                        link(ins, alone=True)
                aggregate(link, first, count)

            def aggregate(link, first=0, count=SUB):
                for j in range(count):
                    ins = v.bn_aggr(mv[:, first + j, :], bst[:, j, :])
                    if j < count - 1:
                        link.count(ins)
                    else:
                        link(ins)

            def variance(link, out, j0, j1, second):
                e = (1.0 + EPS, EPS * EPS) if second else (1.0, EPS)
                link(v.tensor_scalar(out, mv[:, j0:j1, 1], *e, ALU.mult, ALU.add))

            link = Steps(dve, pro, 0)

            def norms(j0, j1):
                stats(link, lambda j: x_sb[:, j0 + j, :], j0, j1 - j0)
                for n in (0, 1):
                    variance(link, var12[:, n, j0:j1], j0, j1, n)
                rsqrt(link, var12[:, :, j0:j1], fac12[:, :, j0:j1], fac_t[:, :, j0:j1])
                if j0 == 0:
                    dve.wait_ge(in_const, 3 * 16)
                    v.tensor_copy(lnb_all[:], col(V_LNB).to_broadcast([P, P])).then_inc(setup, 1)
                link(v.tensor_tensor(fac2[:, j0:j1], fac12[:, 0, j0:j1], var12[:, 0, j0:j1], ALU.mult))
                link(v.tensor_tensor(fac2[:, j0:j1], fac2[:, j0:j1], fac12[:, 1, j0:j1], ALU.mult))

            def tokens(b):
                wait(dve, hT_mm, b)
                for j in range(b * SUB, (b + 1) * SUB):
                    v.tensor_scalar(tok[:, j % SUB, :], x_sb[:, j, :], mv[:, j, 0:1], fac12[:, 0, j:j + 1],
                                    ALU.subtract, ALU.mult).then_inc(h_ready, 1)

            def set_up():
                dve.wait_ge(bias_mm, 1)
                v.tensor_copy(b_qk[:], GB[:, 0:2 * D]).then_inc(setup, 1)
                v.tensor_scalar(w_qkv[:, 0:2 * D], w_qkv[:, 0:2 * D], col(V_LNW), None, ALU.mult).then_inc(setup, 1)

            def gate_weights():
                v.tensor_copy(gq16[:, 0:1], col(V_GQ)).then_inc(setup, 1)
                dve.wait_ge(setup, 6)
                link(v.tensor_tensor(gq_parts[:, 0:1], col(V_GQ), gq16[:, 0:1], ALU.subtract))
                link(v.tensor_copy(gq16[:, 1:2], gq_parts[:, 0:1]))
                link(v.tensor_tensor(gq_parts[:, 1:2], gq_parts[:, 0:1], gq16[:, 1:2], ALU.subtract))
                link(v.tensor_copy(gq16[:, 2:3], gq_parts[:, 1:2]))
                link(v.tensor_copy(gq_parts[:, 2:5], gq16[:, 0:3]))
                link(v.tensor_scalar(gm_t[:], const_sb[:, C_MA:C_MA + P], gq_parts[:, 2:3], None, ALU.mult))
                v.scalar_tensor_tensor(out=gm_a[:], in0=const_sb[:, C_MB:C_MB + P], scalar=gq_parts[:, 3:4], in1=gm_t[:],
                                       op0=ALU.mult, op1=ALU.add).then_inc(setup, 1)
                v.tensor_scalar(gm_b[:], const_sb[:, C_MA:C_MA + P], gq_parts[:, 4:5], None, ALU.mult).then_inc(setup, 1)

            unit_k = qk[:, 1, :].rearrange("p (n d) -> p n d", d=HD)
            unit_q = qk[:, 0, :].rearrange("p (n d) -> p n d", d=HD)

            def unit(b):
                wait(dve, hi_ready, b * 2)
                wait(dve, lo_ready, b * 2)
                for j in range(SUB):
                    dve.wait_ge(raw_ready, b * SUB + j + 1)
                    v.scalar_tensor_tensor(
                        out=qk[:, :, j * D:(j + 1) * D], in0=raw[b % 2][:, j, 0:2 * D].rearrange("p (w n) -> p w n", w=2),
                        scalar=fac2[:, b * SUB + j:b * SUB + j + 1], in1=b_qk[:].rearrange("p (w n) -> p w n", w=2),
                        op0=ALU.mult, op1=ALU.add).then_inc(qk_ready, 1)
                dve.wait_ge(qk_ready, b * SUB + SUB)
                gk = vec_sb[:, V_GK:V_GK + HD].unsqueeze(1).to_broadcast([P, SUB * H, HD])
                link(v.tensor_tensor(gk_prod[:], unit_k, gk, ALU.mult))
                link(v.tensor_reduce(gk_s[:], gk_prod[:], AX_X, ALU.add))
                if 0 < b < NB - 1:
                    tokens(b + 1)
                dve.wait_ge(sq_ready, b + 1)
                link(v.tensor_reduce(ssq[:], sq, AX_X, ALU.add))
                link(v.tensor_scalar(ssq[:], ssq[:], NORM_EPS * NORM_EPS, None, ALU.max))
                rsqrt(link, ssq[:], rn[:], rn_t[:])
                link.count(v.tensor_tensor(gk_s[:], gk_s[:], rn[:, NQK // 2:NQK], ALU.mult))
                link(v.tensor_scalar(rn_t[:], rn[:], QK_SCALE, None, ALU.mult))
                both = qk.rearrange("p w n -> p (w n)").rearrange("p (n d) -> p n d", d=HD)
                v.tensor_tensor(both, both, rn_t[:].unsqueeze(2).to_broadcast([P, NQK, HD]), ALU.mult).then_inc(unit_ready, 1)

            def gated_values(b):
                v.tensor_tensor(vg[:, b * SUB:(b + 1) * SUB, :, :],
                                raw[b % 2][:, :, 2 * D:3 * D].rearrange("p s (h d) -> p s h d", d=HD),
                                gk_s[:].rearrange("p (s h) -> p s h", s=SUB).unsqueeze(3).to_broadcast([P, SUB, H, HD]),
                                ALU.mult).then_inc(vg_ready, 1)

            def low_parts(b):
                for w, of in ((0, unit_q), (1, unit_k)):
                    dve.wait_ge(hi_ready, b * 2 + w + 1)
                    v.tensor_tensor(split[:, w, :, LOW_SLOT[w], :], of, split[:, w, :, 0, :], ALU.subtract).then_inc(lo_ready, 1)

            dve.wait_ge(in_x, 16)
            norms(0, SUB)
            tokens(0)
            set_up()
            dve.wait_ge(in_xs, 16)
            norms(SUB, ST)
            tokens(1)
            for b in range(NB):
                unit(b)
                gated_values(b)
                low_parts(b)
            gate_weights()
            dve.wait_ge(q_saved, (NB - 1) * 16)
            for n in range(4):
                dve.wait_ge(qk_tr, (NB - 1) * 4 + n + 1)
                v.tensor_copy(*turned_bank(NB - 1, n)).then_inc(qk_copied, 1)

            def collapse(i, g):
                dve.wait_ge(av_mm, i * ROUNDS + (g + 1) * ST)
                dve.wait_ge(gateb_copied, i * NG + g + 1)
                if g == 0:
                    wait(dve, proj_mm, i)
                v.tensor_tensor(coll[:, g, :], AV[:], gate_q[:], ALU.mult).then_inc(coll_ready, 1)

            def attention_out(i, link):
                dve.wait_ge(proj_mm, i)
                sums = []
                for j in range(SUB + 1):
                    if j < SUB:
                        link.count(v.tensor_tensor(tok[:, j, :], OB[:, j * D:(j + 1) * D], vec_sb[:, V_BO:V_BO + D], ALU.add))
                        sums.append(link.n)
                    if j > 0:
                        link.after(sums[j - 1])
                        link.count(v.bn_stats(bst[:, j - 1, :], tok[:, j - 1, :]))
                link.after(link.n)
                dve.memset(pause[:], 0.0)
                aggregate(link)
                variance(link, s_var, 0, SUB, False)
                rsqrt(link, s_var, s_fac, s_t)
                for j in range(SUB):
                    ins = v.tensor_scalar(tok[:, j, :], tok[:, j, :], mv[:, j, 0:1], s_fac[:, j:j + 1], ALU.subtract, ALU.mult)
                    if j < SUB - 1:
                        link.count(ins)
                    else:
                        link(ins)
                link(v.tensor_tensor(x1, tok[:], x_sb[:, bass.ds((i - 1) * SUB, SUB), :], ALU.add))
                stats(link, lambda j: x1[:, j, :])
                variance(link, s_var, 0, SUB, True)
                rsqrt(link, s_var, s_fac, s_t)
                for j in range(SUB):
                    ins = v.tensor_scalar(tok[:, j, :], x1[:, j, :], mv[:, j, 0:1], s_fac[:, j:j + 1], ALU.subtract, ALU.mult)
                    if j < SUB - 1:
                        link.count(ins)
                    else:
                        ins.then_inc(n2_ready, 1)

            def expert_in(i):
                dve.wait_ge(n2_mm, i)
                dve.wait_ge(out_saved, i * 16)
                v.tensor_scalar(xnT, UB, col(V_GAM), col(V_BET), ALU.mult, ALU.add).then_inc(xn_ready, 1)
                dve.wait_ge(xn_ready, i * 3 - 2)
                v.tensor_copy(xn_hi[:], xnT).then_inc(xn_ready, 1)
                dve.wait_ge(xn_ready, i * 3 - 1)
                v.tensor_tensor(xn_lo[:], xnT, xn_hi[:].bitcast(F32), ALU.subtract).then_inc(xn_ready, 1)

            def choose(i, link):
                dve.wait_ge(router_mm, i)
                link(v.tensor_copy(logit[:], OB[:, 0:SUB * E].rearrange("p (s e) -> p s e", s=SUB)), alone=True)
                for j in range(SUB):
                    ins = v.max(top[:, j, :], logit[:, j, :])
                    if j < SUB - 1:
                        link.count(ins)
                    else:
                        link(ins)
                v.tensor_tensor(tdiff[:], top[:, :, 1], top[:, :, 0], ALU.subtract).then_inc(diff_ready, 1)
                for j in range(SUB):
                    ins = v.max_index(topi[:, j, :], top[:, j, :], logit[:, j, :])
                    if j < SUB - 1:
                        link.count(ins)
                    else:
                        link(ins)
                link(v.tensor_copy(topf[:], topi[:, :, 0:2]))
                for n in (0, 1):
                    link(v.tensor_tensor(hot[:, n], iota.unsqueeze(1).to_broadcast([P, SUB, E]),
                                         topf[:, :, n:n + 1].to_broadcast([P, SUB, E]), ALU.is_equal))

            def combine(i, link):
                dve.wait_ge(twt_ready, i * 2)
                for n in (0, 1):
                    link(v.tensor_tensor(hot[:, n], hot[:, n], twt[:, n, :].unsqueeze(2).to_broadcast([P, SUB, E]), ALU.mult))
                v.tensor_tensor(hot[:, 2], hot[:, 0], hot[:, 1], ALU.add).then_inc(comb_ready, 1)

            def keep_comb(i):
                dve.wait_ge(combT_mm, i)
                v.tensor_copy(combT, OB[0:E, :]).then_inc(combT_ready, 1)

            def hidden(i, c, part):
                n = (i - 1) * NCH + c
                if part == 0:
                    dve.wait_ge(gate_mm, n + 1)
                    if c >= 2:
                        dve.wait_ge(sg_ready, n - 1)
                    v.tensor_scalar(gate_c[c % 2], gate_bank(i, c), 10.0, -10.0, ALU.min, ALU.max).then_inc(gate_clipped, 1)
                else:
                    dve.wait_ge(up_mm, n + 1)
                    dve.wait_ge(gate_clipped, n + 1)
                    if c >= 2:
                        dve.wait_ge(hid_ready, n - 1)
                    v.tensor_tensor(prod[c % 2], gate_c[c % 2], up_bank(i, c), ALU.mult).then_inc(prod_ready, 1)

            def hidden_low(i, c):
                dve.wait_ge(hid_high, (i - 1) * NCH + c + 1)
                v.tensor_tensor(hid_lo[:, c % LAG], hid[c % 2], hid_hi[:, c % LAG].bitcast(F32), ALU.subtract).then_inc(hid_split, 1)

            def drain(i, n, link):
                c = NCH - LAG + n
                if n < 2:
                    hidden_low(i, NCH - 2 + n)
                if added_after(c) is not None:
                    add_expert(i, added_after(c), link)

            def chunk_part(i, c, part, link):
                if part == 0:
                    hidden(i, c, 0)
                elif part == 1:
                    if c >= 2:
                        hidden_low(i, c - 2)
                    if c >= LAG and added_after(c - LAG) is not None:
                        add_expert(i, added_after(c - LAG), link)
                else:
                    hidden(i, c, 2)
                    if c == COMB_CHUNK:
                        keep_comb(i)

            def add_expert(i, e, link):
                n = (i - 1) * (E + 1)
                dve.wait_ge(down_mm, (i - 1) * NCH + min((e + 1) * FC, NCH))
                if e < E:
                    dve.wait_ge(comb_in[e % 2], ((i - 1) * (E // 2) + e // 2 + 1) * 16)
                if e == 0:
                    v.tensor_tensor(acc, out_bank(i, e), comb_all[:, 0, :], ALU.mult).then_inc(acc_ready, 1)
                elif e < E:
                    link(v.tensor_tensor(tmp, out_bank(i, e), comb_all[:, e % 2, :], ALU.mult))
                    dve.wait_ge(acc_ready, n + e)
                    v.tensor_tensor(acc, acc, tmp, ALU.add).then_inc(acc_ready, 1)
                else:
                    dve.wait_ge(acc_ready, n + e)
                    v.tensor_tensor(acc, acc, out_bank(i, e), ALU.add).then_inc(acc_ready, 1)

            def finish(i, link):
                dve.wait_ge(fin_mm, i)
                stats(link, lambda j: UB[:, j * P:(j + 1) * P])
                variance(link, s_var, 0, SUB, False)
                rsqrt(link, s_var, s_fac, s_t)
                for j in range(SUB):
                    v.tensor_scalar(tok[:, j, :], UB[:, j * P:(j + 1) * P], mv[:, j, 0:1], s_fac[:, j:j + 1],
                                    ALU.subtract, ALU.mult).then_inc(fin_read, 1)
                dve.wait_ge(fin_read, i * SUB)
                v.tensor_tensor(result, tok[:], x1, ALU.add).then_inc(out_ready, 1)

            def gates(i, g):
                dve.wait_ge(gateb_mm, i * NG + g + 1)
                wait(dve, coll_ready, i * NG + g)
                v.tensor_scalar(gate_q[:], GB[:], 1.0 / QK_SCALE, None, ALU.mult).then_inc(gateb_copied, 1)

            def rounds(i, experts):
                link = Steps(dve, blk, (i - 1) * BLK_STEPS) if experts else None
                for k in range(ROUNDS):
                    if experts:
                        if k == 0:
                            attention_out(i, link)
                        if k == TURN_ROUND:
                            expert_in(i)
                        if k == ROUTE_ROUND:
                            choose(i, link)
                            combine(i, link)
                        for c in range(NCH):
                            for part in range(3):
                                if unit_round(c, part) == k:
                                    chunk_part(i, c, part, link)
                        if LAST_UNIT < k <= LAST_UNIT + LAG:
                            drain(i, k - LAST_UNIT - 1, link)
                        if k == FINISH_ROUND:
                            finish(i, link)
                    if k % ST == 0 and k > 0:
                        collapse(i, k // ST - 1)
                    if k % ST == ST - 1:
                        gates(i, k // ST)
                collapse(i, NG - 1)
                if experts:
                    assert link.n == BLK_STEPS, link.n

            rounds(0, False)
            with dve.Fori(1, NB) as i:
                rounds(i, True)
            link = Steps(dve, blk, (NB - 1) * BLK_STEPS)
            attention_out(NB, link)
            expert_in(NB)
            choose(NB, link)
            combine(NB, link)
            for c in range(NCH):
                for part in range(3):
                    chunk_part(NB, c, part, link)
            for n in range(LAG):
                drain(NB, n, link)
            finish(NB, link)


def _layout(inputs):
    import numpy as np

    a = {k[3:]: np.asarray(v) for k, v in inputs.items()}
    f = np.float32
    rows = np.arange(P)
    same_head = rows[:, None] // 32 == rows[None, :] // 32
    first = (rows[:, None] % 32) < 16
    consts = np.concatenate([np.eye(P), same_head & first, same_head & ~first,
                             np.broadcast_to(np.arange(E), (P, E))], axis=1).astype(f)
    gq = np.tile(a["attn_gq"], P // HD)[:, None]
    gk = np.broadcast_to(a["attn_gk"], (P, HD))
    bo = np.broadcast_to(a["attn_bo"], (P, D))
    vecs = np.concatenate([a["attn_ln_w"][:, None], a["attn_ln_b"][:, None], a["ffn_ln_gamma"][:, None],
                           a["ffn_ln_beta"][:, None], gq, gk, bo], axis=1)
    wo = np.zeros((G, 32, NG, D), f)
    wo[:, :HD] = a["attn_Wo"].reshape(NG, G, HD, D).transpose(1, 2, 0, 3)
    gu = np.concatenate([a["ffn_gate_up_w"].transpose(1, 0, 2).reshape(D, E * 2 * F), a["ffn_shared_gate_up_w"]], axis=1)
    down = np.concatenate([a["ffn_down_w"].reshape(E * FC, P, D), a["ffn_shared_down_w"][None]]).transpose(1, 0, 2)
    return {
        "x": a["attn_x"].reshape(ST, P, D).transpose(1, 0, 2),
        "wqkv": np.concatenate([a["attn_Wq"], a["attn_Wk"], a["attn_Wv"]], axis=1),
        "vecs": vecs, "consts": consts, "ident16": np.eye(P, dtype=np.float16),
        "wo": wo.reshape(P, NG, D), "router": a["ffn_router_w"], "gu": gu, "down": down,
    }


def kernel(**inputs):
    import numpy as _np
    import concourse.bacc as _bacc
    from concourse import mybir as _mybir
    from concourse.bass_utils import run_bass_kernel_spmd as _run

    nc = _bacc.Bacc("TRN2", target_bir_lowering=False, num_devices=1)
    arrays, args = {}, []
    for name, a in _layout(inputs).items():
        a = _np.ascontiguousarray(a)
        arrays[f"in_{name}"] = a
        args.append(nc.dram_tensor(f"in_{name}", a.shape, _mybir.dt.from_np(a.dtype), kind="ExternalInput").ap())
    args.append(nc.dram_tensor("out_0", (P, ST, D), _mybir.dt.float32, kind="ExternalOutput").ap())
    build(nc, *args)
    r = _run(nc, [arrays], core_ids=[0])
    got = r.results[0]["out_0"]
    return got.transpose(1, 0, 2).reshape(1, T, D)
```
